# Optimizing a Trainium2 kernel written in Bass

```python
import numpy as np
import jax
import jax.numpy as jnp

def _softmax(x, axis=-1):
    return jax.nn.softmax(x, axis=axis)
def _gelu(x):
    return jax.nn.gelu(x, approximate=True)
def _silu(x):
    return jax.nn.silu(x)
def _sigmoid(x):
    return jax.nn.sigmoid(x)
def _layernorm(x, axis=-1, eps=1e-5):
    m = jnp.mean(x, axis=axis, keepdims=True)
    v = jnp.var(x, axis=axis, keepdims=True)
    return (x - m) / jnp.sqrt(v + eps)
def _scatter_add(tgt, idx, src, axis=0):
    return tgt.at[idx].add(src)
def _segment_sum(src, seg, n):
    return jax.ops.segment_sum(src, seg, n)

kernel_name = 'mk_conv_preact_d2_conv_nchw128_8fee91'

def setup_inputs(seed: int = 0):
    np.random.seed(seed)
    _w = jnp.asarray
    def _rec_inputs():
        import jax
        import jax.numpy as jnp
        _gk = jax.random.key(seed)
        x = -0.0003929 + 0.9999 * jax.random.normal(jax.random.fold_in(_gk, 1), (32, 128, 64, 64), jnp.float32)
        return x
    x = _rec_inputs()
    def _L0_conv_setup():
        import jax, jax.numpy as jnp
        import numpy as np
        HEADS = 4
        DIM_HEAD = 32
        key = jax.random.key(seed)
        k0, k1, k2, k3 = jax.random.split(key, 4)
        b, C, H, W = (32, 128, 64, 64)
        hidden = HEADS * DIM_HEAD
        x = jax.random.normal(k0, (b, C, H, W), dtype=jnp.float32)
        g = jnp.ones((C,), dtype=jnp.float32)
        w_qkv = jax.random.normal(k1, (3 * hidden, C), dtype=jnp.float32) * 0.05
        mem_kv = jax.random.normal(k2, (2, HEADS, DIM_HEAD, 4), dtype=jnp.float32)
        w_out = jax.random.normal(k3, (C, hidden), dtype=jnp.float32) * 0.05
        b_out = jnp.zeros((C,), dtype=jnp.float32)
        return {'x': x, 'g': g, 'w_qkv': w_qkv, 'mem_kv': mem_kv, 'w_out': w_out, 'b_out': b_out}
    _L0_conv_all = _L0_conv_setup()
    _L0_conv_in = {k: v for k, v in _L0_conv_all.items() if k in ('g', 'w_qkv', 'mem_kv', 'w_out', 'b_out', )}
    del _L0_conv_all

    def _L1_conv_setup():
        import jax, jax.numpy as jnp
        import numpy as np
        key = jax.random.key(seed)
        k1, k2, k3, k4 = jax.random.split(key, 4)
        B, I, O, H, W, p = (16, 128, 128, 128, 128, 4)
        x = jax.random.normal(k1, (B, I, H, W), dtype=jnp.float32)
        w3 = jax.random.normal(k2, (O, I, 3, 3), dtype=jnp.float32) * 0.05
        w1 = jax.random.normal(k3, (O, I), dtype=jnp.float32) * 0.05
        b = jax.random.normal(k4, (O, I), dtype=jnp.float32) * 0.05
        return {'x': x, 'w3': w3, 'w1': w1, 'b': b, 'p': p}
    _L1_conv_all = _L1_conv_setup()
    _L1_conv_in = {k: v for k, v in _L1_conv_all.items() if k in ('w3', 'w1', 'b', )}
    del _L1_conv_all

    return {
        "x": x,
        "L0_conv_g": _L0_conv_in["g"],
        "L0_conv_w_qkv": _L0_conv_in["w_qkv"],
        "L0_conv_mem_kv": _L0_conv_in["mem_kv"],
        "L0_conv_w_out": _L0_conv_in["w_out"],
        "L0_conv_b_out": _L0_conv_in["b_out"],
        "L1_conv_w3": _L1_conv_in["w3"],
        "L1_conv_w1": _L1_conv_in["w1"],
        "L1_conv_b": _L1_conv_in["b"],
    }

def reference(x, L0_conv_g, L0_conv_w_qkv, L0_conv_mem_kv, L0_conv_w_out, L0_conv_b_out, L1_conv_w3, L1_conv_w1, L1_conv_b):
    import jax
    import jax.numpy as jnp
    def _L0_conv_ref(x, g, w_qkv, mem_kv, w_out, b_out):
        import jax, jax.numpy as jnp
        import numpy as np
        HEADS = 4
        DIM_HEAD = 32
        b, C, H, W = x.shape
        heads = mem_kv.shape[1]
        dh = mem_kv.shape[2]
        hidden = heads * dh
        scale = dh ** (-0.5)
        norm = jnp.maximum(jnp.sqrt(jnp.sum(x * x, axis=1, keepdims=True)), 1e-12)
        xn = x / norm * g[None, :, None, None] * C ** 0.5
        qkv = jnp.einsum('bchw,oc->bohw', xn, w_qkv)
        q, k, v = jnp.split(qkv, 3, axis=1)
        n = H * W
        q = q.reshape(b, heads, dh, n)
        k = k.reshape(b, heads, dh, n)
        v = v.reshape(b, heads, dh, n)
        mk = jnp.broadcast_to(mem_kv[0][None], (b, heads, dh, mem_kv.shape[3]))
        mv = jnp.broadcast_to(mem_kv[1][None], (b, heads, dh, mem_kv.shape[3]))
        k = jnp.concatenate([mk, k], axis=-1)
        v = jnp.concatenate([mv, v], axis=-1)
        q = jax.nn.softmax(q, axis=-2) * scale
        k = jax.nn.softmax(k, axis=-1)
        context = jnp.einsum('bhdn,bhen->bhde', k, v)
        out = jnp.einsum('bhde,bhdn->bhen', context, q)
        out = out.reshape(b, hidden, H, W)
        return jnp.einsum('bchw,oc->bohw', out, w_out) + b_out[None, :, None, None]

    def _L1_conv_ref(x, w3, w1, b, p):
        import jax, jax.numpy as jnp
        import numpy as np
        O, I = (w3.shape[0], w3.shape[1])
        i = jnp.arange(O)[:, None]
        j = jnp.arange(I)[None, :]
        m3 = (j - i) % p == 0
        w3m = w3 * m3[:, :, None, None].astype(w3.dtype)
        out = jax.lax.conv_general_dilated(x, w3m, window_strides=(1, 1), padding=((1, 1), (1, 1)), dimension_numbers=('NCHW', 'OIHW', 'NCHW'))
        w1m = w1 * (~m3).astype(w1.dtype)
        out = out + jnp.einsum('oi,bihw->bohw', w1m, x)
        out = out + b.sum(axis=1)[None, :, None, None]
        return out

    def _gn(v, G=32, eps=1e-5):
        B_, C_, H_, W_ = v.shape
        g = v.reshape(B_, G, C_ // G, H_, W_)
        m = jnp.mean(g, axis=(2, 3, 4), keepdims=True)
        s = jnp.var(g, axis=(2, 3, 4), keepdims=True)
        return ((g - m) / jnp.sqrt(s + eps)).reshape(v.shape)

    def _ln_c(v, eps=1e-6):
        m = jnp.mean(v, axis=1, keepdims=True)
        s = jnp.var(v, axis=1, keepdims=True)
        return (v - m) / jnp.sqrt(s + eps)

    def _ln_t(v, eps=1e-5):
        m = jnp.mean(v, axis=-1, keepdims=True)
        s = jnp.var(v, axis=-1, keepdims=True)
        return (v - m) / jnp.sqrt(s + eps)

    def _to_tokens(v):
        B_, C_, H_, W_ = v.shape
        return v.reshape(B_, C_, H_ * W_).transpose(0, 2, 1)
    def _from_tokens(t, like):
        B_, C_, H_, W_ = like.shape
        return t.transpose(0, 2, 1).reshape(B_, C_, H_, W_)

    x = x + _L0_conv_ref(_gn(x), L0_conv_g, L0_conv_w_qkv, L0_conv_mem_kv, L0_conv_w_out, L0_conv_b_out)
    x = x + _L1_conv_ref(_gn(x), L1_conv_w3, L1_conv_w1, L1_conv_b, 4)
    return x


_drawn_inputs = setup_inputs


def setup_inputs(seed=0):
    import zlib

    import numpy as np

    out = dict(_drawn_inputs(seed))
    spreads = {'L0_conv_g': (1.0, 0.6), 'L0_conv_b_out': (0.0, 0.33)}
    factors = {'L0_conv_w_qkv': 8.0, 'L0_conv_mem_kv': 8.0, 'L0_conv_w_out': 8.0}
    for name, (base, spread) in spreads.items():
        noise = np.random.default_rng([zlib.crc32(name.encode()), seed]).standard_normal(out[name].shape)
        drawn = base * np.exp(spread * noise) if base else spread * noise
        out[name] = jnp.asarray(drawn.astype(out[name].dtype))
    for name, factor in factors.items():
        out[name] = (out[name] * factor).astype(out[name].dtype)
    return out
```

```python
from contextlib import ExitStack

import concourse.bass as bass
from concourse import mybir

ALU = mybir.AluOpType
ACT = mybir.ActivationFunctionType
AX = mybir.AxisListType
F32 = mybir.dt.float32
F16 = mybir.dt.float16
BF16 = mybir.dt.bfloat16

P = 128
SIDE = 64
PIX = SIDE * SIDE
BANK = 512
CHUNKS = PIX // BANK
UNIT = 2 * BANK
UNITS = PIX // UNIT
BLOCKS = PIX // P
UB = UNIT // P
RES = 4
HEADS = 4
DH = 32
MEM = 4
PAD = SIDE + 2
ROWS = BANK // SIDE
UROWS = UNIT // SIDE
TAPS = 9
GN_EPS = 1e-5
W_SCALE = 64.0
LN_SCALE = 2.0 ** 40
LN2 = 0.6931471805599453
POOL_STEPS = 20
SETUP_READY = 13
WEIGHT_DMAS = 1 + 4 * RES
COL_DMAS = 2 + 2 * RES
X_STEPS = 10
Y_STEPS = 13


def at(sample, per, n):
    pair, offset = sample
    if pair is None:
        return offset * per + n
    return pair * (2 * per) + (offset * per + n)


def build(nc, x, g, w_qkv, mem_kv, w_out, b_out, w3, w1, b1, out):
    batch = x.shape[0]
    x_dram = x.rearrange("b (i r) h w -> b r i (h w)", r=RES)
    out_dram = out.rearrange("b (i r) h w -> b r i (h w)", r=RES)

    with ExitStack() as ctx:
        ctx.enter_context(nc.allow_low_precision(reason="bf16 carries only shifts of softmaxes and exact parts"))
        ctx.enter_context(nc.allow_non_contiguous_dma(reason="small weights in permuted order"))

        def sb(name, shape, dt=F32):
            return ctx.enter_context(nc.sbuf_tensor(name, shape, dt))

        def sem(name):
            return ctx.enter_context(nc.semaphore(name))

        conv_ps = ctx.enter_context(nc.psum_tensor("conv_ps", [P, 2, BANK], F32))
        sum_ps = ctx.enter_context(nc.psum_tensor("sum_ps", [P, BANK], F32))
        small_ps = ctx.enter_context(nc.psum_tensor("small_ps", [P, BANK], F32))
        pair_ps = [ctx.enter_context(nc.psum_tensor(f"pair{q}_ps", [P, UNIT], F32)) for q in range(2)]

        X = [sb(f"x{q}", [P, PIX]) for q in range(2)]
        XG = sb("xg", [P, PIX])
        U = sb("u", [P, PIX])
        UB16 = sb("u_bf16", [P, PIX], BF16)
        SQ = sb("sq", [P, 2, UNIT])
        KT = sb("exp_kT", [P, 2, UNIT])
        UT = sb("uT", [P, 2, UB, P + 1])
        EQ = sb("exp_q", [P, PIX])
        Y = sb("y", [P, PIX])
        YG = sb("yg", [P, 2, UNIT])
        HI = sb("yg_hi", [P, PAD, PAD], F16)
        LO = sb("yg_lo", [P, PAD, PAD], F16)
        OUT = sb("out_stage", [P, PIX])
        bn = sb("bn", [P, 2, CHUNKS, 6])
        st = sb("st", [P, 2, 16])
        nrm = sb("nrm", [P, BANK])
        den = sb("den", [P, BANK])
        part_hi = sb("part_hi", [P, BANK], BF16)
        part_mid = sb("part_mid", [P, BANK], BF16)
        rest1 = sb("rest1", [P, BANK])
        rest2 = sb("rest2", [P, BANK])
        R_norm = sb("r_norm", [P, BANK], BF16)
        R_den = sb("r_den", [P, BANK], BF16)
        km = sb("km", [P, 8])
        kneg_bf = sb("kneg_bf", [P, 2], BF16)
        kneg = sb("kneg", [P, 1])
        krow = sb("krow", [P, 4, P], BF16)
        pk = sb("pk", [P, MEM])
        pk_sum = sb("pk_sum", [P, 1])
        z = sb("z", [P, 2])
        qm = sb("qm", [P, P], BF16)
        qmT = sb("qmT", [P, P], BF16)
        A_sb = sb("a_sb", [P, P + MEM])
        AT_sb = sb("at_sb", [P, P])
        pkT_sb = sb("pkT_sb", [P, P])
        ctxT_sb = sb("ctxT_sb", [P, P])
        MT_sb = sb("mt_sb", [P, P])
        ident = sb("ident", [P, P])
        ident_bf = sb("ident_bf", [P, P], BF16)
        ones_bf = sb("ones_bf", [P, P], BF16)
        same_group = sb("same_group", [P, P])
        head_mask = sb("head_mask", [P, P])
        quad_mask = sb("quad_mask", [P, P])
        other_mask = sb("other_mask", [P, P])
        red_norm = sb("red_norm", [P, 2, 32])
        red_head = sb("red_head", [P, 2, 32])
        spread = sb("spread", [P, CHUNKS, P], BF16)
        minus_max = sb("minus_max", [P, BLOCKS, P], BF16)
        part_grid = sb("part_grid", [P, 4, 4, 8])
        part_mask = sb("part_mask", [P, 4])
        mk = sb("mk", [P, MEM])
        mv = sb("mv", [P, MEM])
        mvT = sb("mvT", [P, P])
        wqkvT = sb("wqkvT", [P, 3, P])
        wqkT_bf = sb("wqkT_bf", [P, 2, P], BF16)
        woT = sb("woT", [P, P])
        gcol = sb("gcol", [P, 1])
        bo = sb("bo", [P, 1])
        b1s = sb("b1s", [P, 1])
        b01 = sb("b01", [P, 1])
        w_hi = sb("w_hi", [P, TAPS, P], F16)
        w_lo = sb("w_lo", [P, TAPS, P], F16)
        idle = sb("idle", [P, 4])
        zcol = sb("zcol", [P, 3])

        raw_qkv = EQ[:, 0:3 * P].rearrange("p (t c) -> p t c", t=3)
        raw_out = EQ[:, 3 * P:4 * P]
        raw_b1 = EQ[:, 4 * P:5 * P]
        raw_w1 = EQ[:, 5 * P:6 * P]
        raw_w3 = EQ[:, 6 * P:15 * P]
        perm_qkv = OUT[:, 0:3 * P].rearrange("p (t r i) -> p t r i", t=3, r=RES)
        perm_w3 = OUT[:, 3 * P:12 * P].rearrange("p (t r i) -> p t r i", t=TAPS, r=RES)
        perm_w1 = OUT[:, 12 * P:13 * P].rearrange("p (r i) -> p r i", r=RES)
        tap32 = OUT[:, 13 * P:23 * P].rearrange("p (t c) -> p t c", t=TAPS + 1)

        x_in = [sem(f"x_in{q}") for q in range(2)]
        weights_in = sem("weights_in")
        stored = [sem(f"stored{u}") for u in range(UNITS)]
        col_in = sem("col_in")
        const_made = sem("const_made")
        setup_pe = sem("setup_pe")
        setup_dve = sem("setup_dve")
        x_stat = sem("x_stat")
        x_stat_act = sem("x_stat_act")
        x_group = sem("x_group")
        y_stat = sem("y_stat")
        y_stat_act = sem("y_stat_act")
        y_group = sem("y_group")
        xg_ready = sem("xg_ready")
        sq_ready = sem("sq_ready")
        norm_sum = sem("norm_sum")
        norm_dve = sem("norm_dve")
        norm_act = sem("norm_act")
        inv_bcast = sem("inv_bcast")
        u_ready = sem("u_ready")
        ub_ready = sem("ub_ready")
        k_rough = sem("k_rough")
        k_max = sem("k_max")
        q_rough = sem("q_rough")
        q_max = sem("q_max")
        max_turned = sem("max_turned")
        pk_ready = sem("pk_ready")
        kT_done = sem("kT_done")
        uT_done = sem("uT_done")
        kT_exp = sem("kT_exp")
        uT_kept = sem("uT_kept")
        ctx_sum = sem("ctx_sum")
        mix_dve = sem("mix_dve")
        mix_pe = sem("mix_pe")
        q_done = sem("q_done")
        q_exp = sem("q_exp")
        den_sum = sem("den_sum")
        den_act = sem("den_act")
        den_dve = sem("den_dve")
        den_bcast = sem("den_bcast")
        q_soft = sem("q_soft")
        mixed = sem("mixed")
        y_ready = sem("y_ready")
        yg_ready = sem("yg_ready")
        hi_ready = sem("hi_ready")
        lo_ready = sem("lo_ready")
        conv_done = sem("conv_done")
        out_ready = sem("out_ready")

        def px(t, v):
            return t[:, v * UNIT:(v + 1) * UNIT]

        def inner(t, v):
            return t[:, 1 + v * UROWS:1 + (v + 1) * UROWS, 1:1 + SIDE]

        def rows(ap):
            return ap.rearrange("p (r c) -> p r c", c=SIDE)

        def first(sample):
            return sample[0] is None and sample[1] == 0

        def index(sample):
            pair, offset = sample
            return offset if pair is None else pair * 2 + offset

        def over_samples(eng, step):
            step((None, 0), None, (None, 1), 1)
            step((None, 1), (None, 0), (None, 2), 0)
            with eng.Fori(1, batch // 2 - 1) as pair:
                step((pair, 0), (pair, -1), (pair, 1), 1)
                step((pair, 1), (pair, 0), (pair, 2), 0)
            step((None, batch - 2), (None, batch - 3), (None, batch - 1), 1)
            step((None, batch - 1), (None, batch - 2), None, 0)
            step(None, (None, batch - 1), None, 0)

        def at_load(sample):
            pair, offset = sample
            loads = 16 * RES
            return loads * (offset // 2 + 1) if pair is None else pair * loads + loads * (offset // 2 + 1)

        def buffer_of(sample):
            return sample[1] % 2

        block = ctx.enter_context(nc.Block())

        @block.sync
        def _(sp):
            def load(s, buf):
                for r in range(RES):
                    sp.dma_start(X[buf][32 * r:32 * r + 32], x_dram[index(s), r]).then_inc(x_in[buf], 16)

            load((None, 0), 0)
            sp.dma_start(raw_qkv, w_qkv.rearrange("(t o) c -> o t c", t=3)).then_inc(weights_in, 16)
            n = 1
            for r in range(RES):
                q = slice(32 * r, 32 * r + 32)
                sp.dma_start(raw_w3[q], w3.rearrange("(i r) c a b -> r i (c a b)", r=RES)[r]).then_inc(weights_in, 16)
                sp.dma_start(raw_w1[q], w1.rearrange("(i r) c -> r i c", r=RES)[r]).then_inc(weights_in, 16)
                sp.dma_start(raw_b1[q], b1.rearrange("(i r) c -> r i c", r=RES)[r]).then_inc(weights_in, 16)
                sp.dma_start(raw_out[q], w_out.rearrange("(i r) c -> r i c", r=RES)[r]).then_inc(weights_in, 16)
                n += 4
            assert n == WEIGHT_DMAS

            def step(a, c, p, pbuf):
                if p is not None:
                    if c is not None:
                        sp.wait_ge(y_ready, at(c, UNITS, UNITS))
                    load(p, pbuf)
                if c is not None:
                    for v in range(UNITS):
                        sp.wait_ge(out_ready, at(c, CHUNKS, 2 * v + 2))
                        for r in range(RES):
                            sp.dma_start(out_dram[index(c), r][:, v * UNIT:(v + 1) * UNIT],
                                         px(OUT, v)[32 * r:32 * r + 32]).then_inc(stored[v], 16)

            over_samples(sp, step)
            for v in range(UNITS):
                sp.wait_ge(stored[v], 16 * RES * batch)

        @block.gpsimd
        def _(pool):
            made = 0

            def make(ins):
                nonlocal made
                ins.then_inc(const_made, 1)
                made += 1
                pool.wait_ge(const_made, made)

            n = 0
            for r in range(RES):
                q = slice(32 * r, 32 * r + 32)
                pool.dma_start(gcol[q], g.rearrange("(i r one) -> r i one", r=RES, one=1)[r]).then_inc(col_in, 16)
                pool.dma_start(bo[q], b_out.rearrange("(i r one) -> r i one", r=RES, one=1)[r]).then_inc(col_in, 16)
                n += 2
            pool.dma_start(mk[:], mem_kv[0].rearrange("h d j -> (h d) j")).then_inc(col_in, 16)
            pool.dma_start(mv[:], mem_kv[1].rearrange("h d j -> (h d) j")).then_inc(col_in, 16)
            assert n + 2 == COL_DMAS
            make(pool.memset(ident[:], 0.0))
            make(pool.affine_select(out=ident[:], in_=ident[:], compare_op=ALU.not_equal, fill=1.0, base=0,
                                    pattern=[[-1, P]], channel_multiplier=1))
            make(pool.tensor_copy(ident_bf[:], ident[:]))
            make(pool.memset(same_group[:], 0.0))
            for k in range(-(RES - 1), RES):
                make(pool.affine_select(out=same_group[:], in_=same_group[:], compare_op=ALU.not_equal,
                                        fill=1.0 / RES, base=32 * k, pattern=[[-1, P]], channel_multiplier=1))
            make(pool.memset(spread[:], 0.0))
            for part in range(4):
                make(pool.affine_select(out=spread[:], in_=spread[:], compare_op=ALU.not_equal, fill=1.0,
                                        base=-8 * part, pattern=[[-4, 2], [-32, 4], [-1, HEADS], [0, DH]],
                                        channel_multiplier=1))
            make(pool.memset(minus_max[:], 0.0))
            make(pool.affine_select(out=minus_max[:], in_=minus_max[:], compare_op=ALU.not_equal, fill=-1.0,
                                    base=0, pattern=[[-4, BLOCKS], [-1, HEADS], [0, DH]], channel_multiplier=1))
            make(pool.memset(part_grid[:], 0.0))
            make(pool.affine_select(out=part_grid[:], in_=part_grid[:], compare_op=ALU.not_equal, fill=1.0,
                                    base=0, pattern=[[-8, 4], [-32, 4], [-1, 8]], channel_multiplier=1))
            assert made == POOL_STEPS
            make(pool.memset(idle[:, 3:4], 0.0))

            def take_wait(column):
                pool.tensor_tensor(idle[:, column:column + 1], idle[:, 3:4], idle[:, 3:4], ALU.add)

            def group_norm_x(p):
                for v in range(UNITS):
                    if v == 0:
                        pool.wait_ge(x_stat, at(p, X_STEPS, X_STEPS))
                    if v == 0:
                        take_wait(0)
                    pool.tensor_scalar(px(XG, v), px(X[0] if buffer_of(p) == 0 else X[1], v), st[:, 0, 9:10],
                                       st[:, 0, 10:11], ALU.mult, ALU.add).then_inc(xg_ready, 1)

            def step(a, c, p, pbuf):
                if c is not None:
                    for v in range(UNITS):
                        if v == 0:
                            pool.wait_ge(y_stat, at(c, Y_STEPS, Y_STEPS))
                        if v >= 2:
                            pool.wait_ge(lo_ready, at(c, UNITS, v - 1))
                        if v != 1:
                            take_wait(v % 3)
                        pool.tensor_scalar(YG[:, v % 2], px(Y, v), st[:, 1, 9:10], st[:, 1, 11:12],
                                           ALU.mult, ALU.add).then_inc(yg_ready, 1)
                if p is not None:
                    group_norm_x(p)

            group_norm_x((None, 0))
            over_samples(pool, step)

        @block.scalar
        def _(act):
            act.wait_ge(setup_dve, SETUP_READY)

            def stat_act(s, per, dve, mine, slot):
                act.wait_ge(dve, at(s, per, 6 if per == X_STEPS else 7))
                act.activation(st[:, slot, 6:7], st[:, slot, 5:6], ACT.Ln, bias=zcol[:, 0:1]).then_inc(mine, 1)
                act.wait_ge(mine, at(s, 2, 1))
                act.activation(st[:, slot, 7:8], st[:, slot, 6:7], ACT.Exp, scale=-0.5,
                               bias=zcol[:, 0:1]).then_inc(mine, 1)

            def square(p, v):
                act.wait_ge(xg_ready, at(p, UNITS, v + 1))
                if v >= 2:
                    act.wait_ge(norm_sum, at(p, UNITS, v - 1))
                act.activation(SQ[:, v % 2], px(XG, v), ACT.Square, bias=zcol[:, 0:1]).then_inc(sq_ready, 1)

            def inverse_norm(p):
                act.wait_ge(norm_dve, at(p, 8, 1))
                act.activation(nrm[:], nrm[:], ACT.Ln, scale=LN_SCALE, bias=zcol[:, 0:1]).then_inc(norm_act, 1)
                act.wait_ge(norm_act, at(p, 2, 1))
                act.activation(nrm[:], nrm[:], ACT.Exp, scale=-0.5, bias=zcol[:, 1:2]).then_inc(norm_act, 1)

            def step(a, c, p, pbuf):
                if a is not None:
                    for v in range(2):
                        act.wait_ge(u_ready, at(a, UNITS, v + 1))
                        act.activation(px(UB16, v), px(U, v), ACT.Copy).then_inc(ub_ready, 1)
                if c is not None:
                    stat_act(c, Y_STEPS, y_stat, y_stat_act, 1)
                if a is not None:
                    for v in range(2, UNITS):
                        act.wait_ge(u_ready, at(a, UNITS, v + 1))
                        act.activation(px(UB16, v), px(U, v), ACT.Copy).then_inc(ub_ready, 1)
                if c is not None:
                    act.wait_ge(y_stat, at(c, Y_STEPS, Y_STEPS))
                    for v in range(UNITS):
                        act.activation(inner(HI, v), rows(px(Y, v)), ACT.Identity, scale=st[:, 1, 9:10],
                                       bias=st[:, 1, 11:12]).then_inc(hi_ready, 1)
                if a is not None:
                    act.wait_ge(k_max, at(a, 8, 7))
                    act.activation(pk[:], mk[:], ACT.Exp, bias=kneg[:], accum_out=pk_sum[:]).then_inc(pk_ready, 1)
                    for v in range(UNITS):
                        act.wait_ge(kT_done, at(a, UNITS, v + 1))
                        if v >= 2:
                            act.wait_ge(ctx_sum, at(a, UNITS, v - 1))
                        act.activation(KT[:, v % 2], pair_ps[0][:], ACT.Exp, bias=zcol[:, 0:1]).then_inc(kT_exp, 1)
                        act.wait_ge(uT_done, at(a, UNITS, v + 1))
                        act.activation(UT[:, v % 2, :, 0:P], pair_ps[1][:].rearrange("p (b c) -> p b c", c=P),
                                       ACT.Copy).then_inc(uT_kept, 1)
                if p is not None:
                    stat_act(p, X_STEPS, x_stat, x_stat_act, 0)
                if a is not None:
                    for v in range(UNITS):
                        act.wait_ge(q_done, at(a, UNITS, v + 1))
                        act.activation(px(EQ, v), pair_ps[v % 2][:], ACT.Exp, bias=zcol[:, 0:1]).then_inc(q_exp, 1)
                if p is not None:
                    square(p, 0)
                    square(p, 1)
                if a is not None:
                    act.wait_ge(den_sum, at(a, 1, 1))
                    act.activation(den[:], sum_ps[:], ACT.Ln, bias=zcol[:, 0:1]).then_inc(den_act, 1)
                    act.wait_ge(den_act, at(a, 2, 1))
                    act.activation(den[:], den[:], ACT.Exp, scale=-1.0, bias=zcol[:, 0:1]).then_inc(den_act, 1)
                if p is not None:
                    square(p, 2)
                    square(p, 3)
                    inverse_norm(p)

            stat_act((None, 0), X_STEPS, x_stat, x_stat_act, 0)
            for v in range(UNITS):
                square((None, 0), v)
            inverse_norm((None, 0))
            over_samples(act, step)

        @block.tensor
        def _(pe):
            pe.wait_ge(const_made, POOL_STEPS)
            pe.wait_ge(col_in, 16 * COL_DMAS)
            pe.wait_ge(setup_dve, 3)
            def turn(dst, src, m=P):
                return pe.transpose(dst, src, ident[:])
            for t in range(3):
                turn(conv_ps[:, 0, t * P:(t + 1) * P], perm_qkv[:, t].rearrange("p r i -> p (r i)"))
            turn(conv_ps[:, 0, 3 * P:4 * P], raw_out)
            pe.transpose(small_ps[0:MEM, 0:P], mv[:], ident[:])
            for t in range(TAPS + 1):
                src = perm_w3[:, t] if t < TAPS else perm_w1
                bank = [pair_ps[0][:, 0:BANK], pair_ps[0][:, BANK:UNIT], pair_ps[1][:, 0:BANK]][t // 4]
                last = turn(bank[:, (t % 4) * P:(t % 4 + 1) * P], src.rearrange("p r i -> p (r i)"))
            last.then_inc(setup_pe, 1)
            pe.wait_ge(setup_dve, SETUP_READY)

            def norm_sums(p, v):
                pe.wait_ge(sq_ready, at(p, UNITS, v + 1))
                for j in (2 * v, 2 * v + 1):
                    t, s = j % 4, j // 4
                    mm = pe.matmul(sum_ps[32 * t:32 * t + 32, :], red_norm[:, s], SQ[:, v % 2, (j % 2) * BANK:(j % 2 + 1) * BANK],
                                   start=(s == 0), stop=(s == 1))
                mm.then_inc(norm_sum, 1)

            def broadcast(R, v, done):
                for j in (2 * v, 2 * v + 1):
                    mm = pe.matmul(pair_ps[v % 2][:, (j % 2) * BANK:(j % 2 + 1) * BANK], spread[:, j], R[:],
                                   start=True, stop=True)
                mm.then_inc(done, 1)

            def inv_norm(a, c, v):
                if v == 0:
                    pe.wait_ge(norm_dve, at(a, 8, 8))
                if v < 2 and c is not None:
                    pe.wait_ge(y_ready, at(c, UNITS, 3 + v))
                if v >= 2:
                    pe.wait_ge(u_ready, at(a, UNITS, v - 1))
                broadcast(R_norm, v, inv_bcast)

            def rough_k(a, v):
                pe.wait_ge(ub_ready, at(a, UNITS, v + 1))
                if v < 2:
                    pe.wait_ge(u_ready, at(a, UNITS, v + 3))
                else:
                    pe.wait_ge(k_max, at(a, 8, v - 1))
                for j in (2 * v, 2 * v + 1):
                    mm = pe.matmul(pair_ps[v % 2][:, (j % 2) * BANK:(j % 2 + 1) * BANK], wqkT_bf[:, 1],
                                   UB16[:, j * BANK:(j + 1) * BANK], start=True, stop=True)
                mm.then_inc(k_rough, 1)

            def rough_q(a, v):
                if v < 2:
                    pe.wait_ge(k_max, at(a, 8, v + 3))
                else:
                    pe.wait_ge(q_max, at(a, 5, v - 1))
                for b in range(UB):
                    c0 = (v * UB + b) * P
                    mm = pe.matmul(pair_ps[v % 2][:, b * P:(b + 1) * P], UB16[:, c0:c0 + P], wqkT_bf[:, 0],
                                   start=True, stop=True)
                mm.then_inc(q_rough, 1)

            def keys(a, v):
                if v == 0:
                    pe.wait_ge(k_max, at(a, 8, 8))
                    pe.wait_ge(q_max, at(a, 5, 3))
                else:
                    pe.wait_ge(kT_exp, at(a, UNITS, v))
                for half in range(2):
                    bank = pair_ps[0][:, half * BANK:(half + 1) * BANK]
                    pe.matmul(bank, ones_bf[:], krow[:].rearrange("p a b -> p (a b)"), start=True, stop=False,
                              skip_group_check=True)
                    for b in range(4):
                        c0 = (v * UB + half * 4 + b) * P
                        mm = pe.matmul(bank[:, b * P:(b + 1) * P], U[:, c0:c0 + P], wqkvT[:, 1],
                                       start=False, stop=(b == 3), skip_group_check=True)
                mm.then_inc(kT_done, 1)

            def turn_u(a, v):
                if v == 0:
                    pe.wait_ge(q_max, at(a, 5, 4))
                else:
                    pe.wait_ge(uT_kept, at(a, UNITS, v))
                for b in range(UB):
                    c0 = (v * UB + b) * P
                    mm = pe.transpose(pair_ps[1][:, b * P:(b + 1) * P], U[:, c0:c0 + P], ident[:])
                mm.then_inc(uT_done, 1)

            def context(a, v):
                pe.wait_ge(kT_exp, at(a, UNITS, v + 1))
                pe.wait_ge(uT_kept, at(a, UNITS, v + 1))
                for b in range(UB):
                    mm = pe.matmul(sum_ps[:, 0:P + 1], KT[:, v % 2, b * P:(b + 1) * P], UT[:, v % 2, b],
                                   start=(v == 0 and b == 0), stop=(v == UNITS - 1 and b == UB - 1))
                mm.then_inc(ctx_sum, 1)

            def queries(a, v):
                if v == 0:
                    pe.wait_ge(q_max, at(a, 5, 5))
                    pe.wait_ge(kT_exp, at(a, UNITS, UNITS))
                elif v == 1:
                    pe.wait_ge(uT_kept, at(a, UNITS, UNITS))
                else:
                    pe.wait_ge(q_exp, at(a, UNITS, v - 1))
                for j in (2 * v, 2 * v + 1):
                    bank = pair_ps[v % 2][:, (j % 2) * BANK:(j % 2 + 1) * BANK]
                    pe.matmul(bank, wqkvT[:, 0], U[:, j * BANK:(j + 1) * BANK], start=True, stop=False,
                              skip_group_check=True)
                    for b in range(4):
                        mm = pe.matmul(bank[:, b * P:(b + 1) * P], minus_max[:, 4 * j + b], qmT[:],
                                       start=False, stop=(b == 3), skip_group_check=True)
                mm.then_inc(q_done, 1)

            def denominators(a):
                pe.wait_ge(mix_dve, at(a, 8, 3))
                for j in range(CHUNKS):
                    t, s = j % 4, j // 4
                    if j % 2 == 0:
                        pe.wait_ge(q_exp, at(a, UNITS, j // 2 + 1))
                    mm = pe.matmul(sum_ps[32 * t:32 * t + 32, :], red_head[:, s], EQ[:, j * BANK:(j + 1) * BANK],
                                   start=(s == 0), stop=(s == 1))
                mm.then_inc(den_sum, 1)

            def den_broadcast(a, v):
                if v < 2:
                    if v == 0:
                        pe.wait_ge(den_dve, at(a, 7, 7))
                    pe.wait_ge(q_exp, at(a, UNITS, v + 3))
                else:
                    pe.wait_ge(y_ready, at(a, UNITS, v - 1))
                broadcast(R_den, v, den_bcast)

            def mix(a, v):
                if v == 0:
                    pe.wait_ge(mix_dve, at(a, 8, 8))
                pe.wait_ge(q_soft, at(a, UNITS, v + 1))
                for j in (2 * v, 2 * v + 1):
                    mm = pe.matmul(pair_ps[v % 2][:, (j % 2) * BANK:(j % 2 + 1) * BANK], MT_sb[:],
                                   EQ[:, j * BANK:(j + 1) * BANK], start=True, stop=True)
                mm.then_inc(mixed, 1)

            def conv(c, j):
                if c is None:
                    return
                last_unit = min(UNITS - 1, (ROWS * (j + 1)) // UROWS)
                pe.wait_ge(lo_ready, at(c, UNITS, last_unit + 1))
                if j >= 2 or not first(c):
                    pe.wait_ge(out_ready, at(c, CHUNKS, max(0, j - 1)))
                n = 0
                for t in range(TAPS):
                    dy, dx = divmod(t, 3)
                    for w, data in ((w_hi, HI), (w_lo, HI), (w_hi, LO)):
                        mm = pe.matmul(conv_ps[:, j % 2], w[:, t], data[:, j * ROWS + dy:(j + 1) * ROWS + dy, dx:dx + SIDE],
                                       start=(n == 0), stop=(n == 3 * TAPS - 1))
                        n += 1
                mm.then_inc(conv_done, 1)

            def step(a, c, p, pbuf):
                if a is not None:
                    inv_norm(a, c, 0)
                    inv_norm(a, c, 1)
                if c is not None:
                    pe.wait_ge(mix_dve, at(c, 8, 8))
                    pe.wait_ge(y_stat, at(c, Y_STEPS, 4))
                    pe.matmul(small_ps[:, 0:2], same_group[:], st[:, 1, 0:2], start=True, stop=True).then_inc(y_group, 1)
                if a is not None:
                    inv_norm(a, c, 2)
                    inv_norm(a, c, 3)
                    rough_k(a, 0)
                    rough_k(a, 1)
                conv(c, 0)
                if a is not None:
                    rough_k(a, 2)
                    rough_k(a, 3)
                    rough_q(a, 0)
                    rough_q(a, 1)
                conv(c, 1)
                if a is not None:
                    rough_q(a, 2)
                    rough_q(a, 3)
                    if c is not None:
                        pe.wait_ge(y_stat, at(c, Y_STEPS, 5))
                    pe.wait_ge(k_max, at(a, 8, 6))
                    pe.transpose(small_ps[0:1, 0:P // 2].bitcast(BF16), kneg_bf[:, 0:1], ident_bf[:]).then_inc(max_turned, 1)
                conv(c, 2)
                if a is not None:
                    pe.wait_ge(k_max, at(a, 8, 8))
                    pe.wait_ge(q_max, at(a, 5, 4))
                    pe.transpose(small_ps[:, 0:P // 2].bitcast(BF16), qm[:], ident_bf[:]).then_inc(max_turned, 1)
                    keys(a, 0)
                    turn_u(a, 0)
                conv(c, 3)
                if a is not None:
                    for v in range(1, 3):
                        keys(a, v)
                        turn_u(a, v)
                        context(a, v - 1)
                conv(c, 4)
                if a is not None:
                    keys(a, 3)
                    turn_u(a, 3)
                    context(a, 2)
                if p is not None:
                    pe.wait_ge(x_stat, at(p, X_STEPS, 3))
                    if a is not None:
                        pe.wait_ge(q_max, at(a, 5, 5))
                    pe.matmul(small_ps[:, 0:2], same_group[:], st[:, 0, 0:2], start=True, stop=True).then_inc(x_group, 1)
                if a is not None:
                    context(a, 3)
                conv(c, 5)
                if a is not None:
                    queries(a, 0)
                    queries(a, 1)
                    pe.wait_ge(mix_dve, at(a, 8, 4))
                    if p is not None:
                        pe.wait_ge(x_stat, at(p, X_STEPS, 4))
                    pe.transpose(small_ps[:, 0:P], A_sb[:, 0:P], ident[:])
                    pe.transpose(small_ps[0:MEM, P:2 * P], A_sb[:, P:P + MEM], ident[:]).then_inc(mix_pe, 1)
                    queries(a, 2)
                    queries(a, 3)
                    pe.wait_ge(mix_dve, at(a, 8, 6))
                    pe.matmul(small_ps[:, 0:P], wqkvT[:, 2], AT_sb[:], start=True, stop=False)
                    pe.matmul(small_ps[:, 0:P], mvT[0:MEM], pkT_sb[0:MEM], start=False, stop=True).then_inc(mix_pe, 1)
                    denominators(a)
                conv(c, 6)
                if a is not None:
                    pe.wait_ge(mix_dve, at(a, 8, 7))
                    pe.matmul(small_ps[:, 0:P], ctxT_sb[:], woT[:], start=True, stop=True).then_inc(mix_pe, 1)
                    den_broadcast(a, 0)
                    den_broadcast(a, 1)
                if p is not None:
                    if a is not None:
                        pe.wait_ge(den_act, at(a, 2, 1))
                    norm_sums(p, 0)
                    norm_sums(p, 1)
                if a is not None:
                    mix(a, 0)
                    mix(a, 1)
                    den_broadcast(a, 2)
                    den_broadcast(a, 3)
                conv(c, 7)
                if p is not None:
                    norm_sums(p, 2)
                    norm_sums(p, 3)
                if a is not None:
                    mix(a, 2)
                    mix(a, 3)

            pe.wait_ge(x_stat, 3)
            pe.matmul(small_ps[:, 0:2], same_group[:], st[:, 0, 0:2], start=True, stop=True).then_inc(x_group, 1)
            for v in range(UNITS):
                norm_sums((None, 0), v)
            over_samples(pe, step)

        @block.vector
        def _(dve):
            made = 0

            def make(ins, wait=False):
                nonlocal made
                ins.then_inc(setup_dve, 1)
                made += 1
                if wait:
                    dve.wait_ge(setup_dve, made)

            dve.wait_ge(weights_in, 16 * WEIGHT_DMAS)
            make(dve.tensor_copy(perm_qkv, raw_qkv.rearrange("p t (i r) -> p t r i", r=RES)))
            make(dve.tensor_copy(perm_w1, raw_w1.rearrange("p (i r) -> p r i", r=RES)))
            for t in range(TAPS):
                last = dve.tensor_copy(perm_w3[:, t], raw_w3.rearrange("p (i r t) -> p t r i", r=RES, t=TAPS)[:, t])
            make(last)
            for t in (ones_bf, UT):
                dve.memset(t[:], 1.0)
            for t in (HI, LO, krow, head_mask, quad_mask, red_norm, red_head):
                last = dve.memset(t[:], 0.0)
            make(last, wait=True)
            dve.memset(other_mask[:], 1.0)
            for h in range(HEADS):
                q = slice(DH * h, DH * h + DH)
                dve.memset(head_mask[q, q], DH ** -0.5)
                dve.memset(quad_mask[q, q], 1.0)
            for s in range(2):
                dve.memset(red_norm[:, s].rearrange("p (part s h) -> p part s h", s=2, h=4)[:, :, s, :], 1.0)
                for h in range(HEADS):
                    q = slice(DH * h, DH * h + DH)
                    dve.memset(red_head[q, s].rearrange("p (part s h) -> p part s h", s=2, h=4)[:, :, s, h:h + 1], 1.0)
            dve.memset(zcol[:, 0:1], 0.0)
            dve.memset(zcol[:, 1:2], 0.5 * (7 + 40) * LN2)
            last = dve.tensor_reduce(b1s[:], raw_b1, AX.X, ALU.add)
            make(last, wait=True)
            for h in range(HEADS):
                q = slice(DH * h, DH * h + DH)
                last = dve.memset(other_mask[q, q], 0.0)
            make(last, wait=True)
            dve.wait_ge(const_made, POOL_STEPS)
            make(dve.tensor_reduce(part_mask[:], part_grid[:].rearrange("p k t w -> p k (t w)"), AX.X, ALU.add))
            dve.wait_ge(col_in, 16 * COL_DMAS)
            dve.tensor_tensor(b01[:], bo[:], b1s[:], ALU.add)
            make(dve.tensor_reduce(km[:, 4:5], mk[:], AX.X, ALU.max))
            dve.wait_ge(setup_pe, 1)
            make(dve.tensor_scalar(wqkvT[:].rearrange("p t c -> p (t c)"), conv_ps[:, 0, 0:3 * P], gcol[:], None,
                                   ALU.mult), wait=True)
            dve.tensor_copy(wqkT_bf[:], wqkvT[:, 0:2])
            dve.tensor_copy(woT[:], conv_ps[:, 0, 3 * P:4 * P])
            dve.tensor_copy(mvT[0:MEM], small_ps[0:MEM, 0:P])
            for t in range(TAPS + 1):
                bank = [pair_ps[0][:, 0:BANK], pair_ps[0][:, BANK:UNIT], pair_ps[1][:, 0:BANK]][t // 4]
                last = dve.scalar_tensor_tensor(out=tap32[:, t], in0=bank[:, (t % 4) * P:(t % 4 + 1) * P], scalar=W_SCALE,
                                                in1=quad_mask[:] if t < TAPS else other_mask[:],
                                                op0=ALU.mult, op1=ALU.mult)
            make(last, wait=True)
            make(dve.tensor_tensor(tap32[:, TAPS // 2], tap32[:, TAPS // 2], tap32[:, TAPS], ALU.add), wait=True)
            make(dve.tensor_copy(w_hi[:], tap32[:, 0:TAPS]), wait=True)
            make(dve.tensor_tensor(w_lo[:], tap32[:, 0:TAPS], w_hi[:], ALU.subtract), wait=True)
            assert made == SETUP_READY, made

            def chain(sem_, sample, per, n):
                def did(ins, wait=True):
                    nonlocal n
                    ins.then_inc(sem_, 1)
                    n += 1
                    if wait:
                        dve.wait_ge(sem_, at(sample, per, n))
                return did

            def channel_stats(src, slot, s, did):
                dve.memset(idle[:, 2:3], 0.0)
                did(dve.bn_aggr(st[:, slot, 0:2], bn[:, slot].rearrange("p c s -> p (c s)")))
                if slot == 1:
                    did(dve.tensor_tensor(st[:, slot, 0:1], st[:, slot, 0:1], b1s[:], ALU.subtract))
                did(dve.scalar_tensor_tensor(out=st[:, slot, 1:2], in0=st[:, slot, 0:1], scalar=st[:, slot, 0:1],
                                             in1=st[:, slot, 1:2], op0=ALU.mult, op1=ALU.add), wait=False)

            def variance(slot, did):
                did(dve.tensor_copy(st[:, slot, 2:4], small_ps[:, 0:2]))
                did(dve.scalar_tensor_tensor(out=st[:, slot, 4:5], in0=st[:, slot, 2:3], scalar=st[:, slot, 2:3],
                                             in1=st[:, slot, 3:4], op0=ALU.mult, op1=ALU.subtract))
                did(dve.tensor_scalar(st[:, slot, 5:6], st[:, slot, 4:5], -1.0, GN_EPS, ALU.mult, ALU.add), wait=False)

            def scale_shift(slot, did):
                did(dve.scalar_tensor_tensor(out=st[:, slot, 8:9], in0=st[:, slot, 7:8], scalar=st[:, slot, 7:8],
                                             in1=st[:, slot, 5:6], op0=ALU.mult, op1=ALU.mult))
                did(dve.tensor_scalar(st[:, slot, 8:9], st[:, slot, 8:9], -0.5, 1.5, ALU.mult, ALU.add))
                did(dve.tensor_tensor(st[:, slot, 9:10], st[:, slot, 8:9], st[:, slot, 7:8], ALU.mult))
                did(dve.tensor_scalar(st[:, slot, 10:11], st[:, slot, 2:3], st[:, slot, 9:10], -1.0,
                                      ALU.mult, ALU.mult), wait=(slot == 1))
                if slot == 1:
                    did(dve.tensor_scalar(st[:, slot, 12:13], b1s[:], st[:, slot, 9:10], -1.0, ALU.mult, ALU.mult))
                    did(dve.tensor_tensor(st[:, slot, 11:12], st[:, slot, 12:13], st[:, slot, 10:11], ALU.add), wait=False)

            def x_stats(p, first):
                if first:
                    dve.wait_ge(x_in[buffer_of(p)], at_load(p))
                for j in range(0 if first else 4, 4 if first else CHUNKS):
                    last = dve.bn_stats(bn[:, 0, j], X[buffer_of(p)][:, j * BANK:(j + 1) * BANK])
                if not first:
                    did = chain(x_stat, p, X_STEPS, 0)
                    did(last)
                    channel_stats(X, 0, p, did)

            def x_variance(p):
                dve.wait_ge(x_group, at(p, 1, 1))
                variance(0, chain(x_stat, p, X_STEPS, 3))

            def x_scale(p):
                dve.wait_ge(x_stat_act, at(p, 2, 2))
                scale_shift(0, chain(x_stat, p, X_STEPS, 6))

            def three_parts(src, R, did):
                did(dve.tensor_copy(part_hi[:], src[:]))
                did(dve.tensor_tensor(rest1[:], src[:], part_hi[:], ALU.subtract))
                did(dve.tensor_copy(part_mid[:], rest1[:]))
                did(dve.tensor_scalar(R[:], part_hi[:], part_mask[:, 0:1], None, ALU.mult))
                did(dve.tensor_tensor(rest2[:], rest1[:], part_mid[:], ALU.subtract))
                did(dve.scalar_tensor_tensor(out=R[:], in0=part_mid[:], scalar=part_mask[:, 1:2], in1=R[:],
                                             op0=ALU.mult, op1=ALU.add))
                did(dve.scalar_tensor_tensor(out=R[:], in0=rest2[:], scalar=part_mask[:, 2:3], in1=R[:],
                                             op0=ALU.mult, op1=ALU.add))

            def norm_guard(p):
                dve.wait_ge(norm_sum, at(p, UNITS, UNITS))
                dve.tensor_scalar(nrm[:], sum_ps[:], 1e-24, None, ALU.max).then_inc(norm_dve, 1)

            def norm_parts(p):
                dve.wait_ge(norm_act, at(p, 2, 2))
                three_parts(nrm, R_norm, chain(norm_dve, p, 8, 1))

            def normalise(a, v):
                dve.wait_ge(inv_bcast, at(a, UNITS, v + 1))
                dve.tensor_tensor(px(U, v), px(XG, v), pair_ps[v % 2][:], ALU.mult).then_inc(u_ready, 1)

            def low_part(c, v):
                dve.wait_ge(yg_ready, at(c, UNITS, v + 1))
                dve.wait_ge(hi_ready, at(c, UNITS, v + 1))
                dve.tensor_tensor(inner(LO, v), rows(YG[:, v % 2]), inner(HI, v), ALU.subtract).then_inc(lo_ready, 1)

            def max_k(a, v):
                dve.wait_ge(k_rough, at(a, UNITS, v + 1))
                dve.tensor_reduce(km[:, v:v + 1], pair_ps[v % 2][:], AX.X, ALU.max).then_inc(k_max, 1)

            def max_q(a, v):
                dve.wait_ge(q_rough, at(a, UNITS, v + 1))
                dve.tensor_reduce(qm[:, v * 32:(v + 1) * 32], pair_ps[v % 2][:].rearrange("p (b d) -> p b d", d=DH),
                                  AX.X, ALU.max).then_inc(q_max, 1)

            def finish(c, j):
                if c is None:
                    return
                if j % 2 == 0 and not first(c):
                    dve.wait_ge(stored[j // 2], at(c, 16 * RES, 0))
                dve.wait_ge(conv_done, at(c, CHUNKS, j + 1))
                dve.scalar_tensor_tensor(out=OUT[:, j * BANK:(j + 1) * BANK], in0=conv_ps[:, j % 2],
                                         scalar=1.0 / W_SCALE, in1=Y[:, j * BANK:(j + 1) * BANK],
                                         op0=ALU.mult, op1=ALU.add).then_inc(out_ready, 1)

            def soften(a, v):
                dve.wait_ge(den_bcast, at(a, UNITS, v + 1))
                dve.tensor_tensor(px(EQ, v), px(EQ, v), pair_ps[v % 2][:], ALU.mult).then_inc(q_soft, 1)

            def residual(a, c, v):
                if c is not None:
                    dve.wait_ge(out_ready, at(c, CHUNKS, 2 * v + 2))
                dve.wait_ge(mixed, at(a, UNITS, v + 1))
                dve.scalar_tensor_tensor(out=px(Y, v), in0=pair_ps[v % 2][:], scalar=b01[:], in1=px(X[buffer_of(a)], v),
                                         op0=ALU.add, op1=ALU.add).then_inc(y_ready, 1)

            def y_bn(a, v):
                dve.wait_ge(y_ready, at(a, UNITS, v + 1))
                for j in (2 * v, 2 * v + 1):
                    last = dve.bn_stats(bn[:, 1, j], Y[:, j * BANK:(j + 1) * BANK])
                return last

            def step(a, c, p, pbuf):
                if a is not None:
                    normalise(a, 0)
                    normalise(a, 1)
                if c is not None:
                    dve.wait_ge(y_group, at(c, 1, 1))
                    variance(1, chain(y_stat, c, Y_STEPS, 4))
                if a is not None:
                    normalise(a, 2)
                    normalise(a, 3)
                if c is not None:
                    dve.wait_ge(y_stat_act, at(c, 2, 2))
                    scale_shift_y(c)
                    low_part(c, 0)
                if a is not None:
                    max_k(a, 0)
                    max_k(a, 1)
                if c is not None:
                    low_part(c, 1)
                finish(c, 0)
                if a is not None:
                    max_k(a, 2)
                    max_k(a, 3)
                    did = chain(k_max, a, 8, 4)
                    dve.wait_ge(k_max, at(a, 8, 4))
                    did(dve.tensor_reduce(km[:, 5:6], km[:, 0:5], AX.X, ALU.max))
                    did(dve.tensor_scalar(kneg_bf[:, 0:1], km[:, 5:6], -1.0, None, ALU.mult))
                    did(dve.tensor_copy(kneg[:], kneg_bf[:, 0:1]), wait=False)
                    max_q(a, 0)
                    max_q(a, 1)
                if c is not None:
                    low_part(c, 2)
                    low_part(c, 3)
                finish(c, 1)
                if a is not None:
                    max_q(a, 2)
                    max_q(a, 3)
                    dve.wait_ge(max_turned, at(a, 2, 1))
                    dve.tensor_copy(krow[0:1], small_ps[0:1, 0:P // 2].bitcast(BF16).unsqueeze(1).to_broadcast([1, 4, P])
                                    ).then_inc(k_max, 1)
                finish(c, 2)
                if a is not None:
                    dve.wait_ge(max_turned, at(a, 2, 2))
                    dve.tensor_copy(qmT[:], small_ps[:, 0:P // 2].bitcast(BF16)).then_inc(q_max, 1)
                if p is not None:
                    x_stats(p, True)
                finish(c, 3)
                if p is not None:
                    x_stats(p, False)
                finish(c, 4)
                if p is not None:
                    x_variance(p)
                if a is not None:
                    dve.wait_ge(ctx_sum, at(a, UNITS, UNITS))
                    dve.wait_ge(pk_ready, at(a, 1, 1))
                    did = chain(mix_dve, a, 8, 0)
                    did(dve.tensor_tensor(z[:, 0:1], sum_ps[:, P:P + 1], pk_sum[:], ALU.add))
                    did(dve.reciprocal(z[:, 1:2], z[:, 0:1]))
                    did(dve.tensor_scalar(A_sb[:, 0:P], sum_ps[:, 0:P], z[:, 1:2], None, ALU.mult), wait=False)
                    did(dve.tensor_scalar(A_sb[:, P:P + MEM], pk[:], z[:, 1:2], None, ALU.mult), wait=False)
                finish(c, 5)
                if p is not None:
                    x_scale(p)
                if a is not None:
                    dve.wait_ge(mix_pe, at(a, 3, 1))
                    did(dve.tensor_copy(AT_sb[:], small_ps[:, 0:P]), wait=False)
                    did(dve.tensor_copy(pkT_sb[0:MEM], small_ps[0:MEM, P:2 * P]), wait=False)
                    dve.wait_ge(mix_pe, at(a, 3, 2))
                    did(dve.tensor_tensor(ctxT_sb[:], small_ps[:, 0:P], head_mask[:], ALU.mult), wait=False)
                    dve.wait_ge(den_act, at(a, 2, 2))
                    three_parts(den, R_den, chain(den_dve, a, 7, 0))
                finish(c, 6)
                if a is not None:
                    dve.wait_ge(mix_pe, at(a, 3, 3))
                    did(dve.tensor_copy(MT_sb[:], small_ps[:, 0:P]), wait=False)
                    soften(a, 0)
                    soften(a, 1)
                    residual(a, c, 0)
                    residual(a, c, 1)
                    soften(a, 2)
                    soften(a, 3)
                    y_bn(a, 0)
                    y_bn(a, 1)
                finish(c, 7)
                if p is not None:
                    norm_guard(p)
                if a is not None:
                    residual(a, c, 2)
                    residual(a, c, 3)
                    y_bn(a, 2)
                    did = chain(y_stat, a, Y_STEPS, 0)
                    did(y_bn(a, 3))
                    channel_stats(Y, 1, a, did)
                if p is not None:
                    norm_parts(p)

            def scale_shift_y(c):
                scale_shift(1, chain(y_stat, c, Y_STEPS, 7))

            x_stats((None, 0), True)
            x_stats((None, 0), False)
            x_variance((None, 0))
            x_scale((None, 0))
            norm_guard((None, 0))
            norm_parts((None, 0))
            over_samples(dve, step)

    return nc


_INS = ['x', 'L0_conv_g', 'L0_conv_w_qkv', 'L0_conv_mem_kv', 'L0_conv_w_out', 'L0_conv_b_out',
        'L1_conv_w3', 'L1_conv_w1', 'L1_conv_b']


def kernel(**inputs):
    import numpy as _np
    import concourse.bacc as _bacc
    from concourse.bass_utils import run_bass_kernel_spmd as _run

    nc = _bacc.Bacc("TRN2", target_bir_lowering=False, num_devices=1)
    arrays, args = {}, []
    for name in _INS:
        a = _np.ascontiguousarray(inputs[name])
        arrays[f"in_{name}"] = a
        args.append(nc.dram_tensor(f"in_{name}", a.shape, mybir.dt.from_np(a.dtype), kind="ExternalInput").ap())
    out = nc.dram_tensor("out", inputs["x"].shape, F32, kind="ExternalOutput").ap()
    build(nc, *args, out)
    r = _run(nc, [arrays], core_ids=[0])
    return r.results[0]["out"]
```

```python
from contextlib import ExitStack

import concourse.bass as bass
from concourse import mybir

ALU = mybir.AluOpType
ACT = mybir.ActivationFunctionType
AX = mybir.AxisListType
F32 = mybir.dt.float32
F16 = mybir.dt.float16
BF16 = mybir.dt.bfloat16

P = 128
SIDE = 64
PIX = SIDE * SIDE
BANK = 512
CHUNKS = PIX // BANK
UNIT = 2 * BANK
UNITS = PIX // UNIT
BLOCKS = PIX // P
UB = UNIT // P
RES = 4
HEADS = 4
DH = 32
MEM = 4
PAD = SIDE + 2
ROWS = BANK // SIDE
UROWS = UNIT // SIDE
SPLIT = PAD // 2 + 1
TAPS = 9
REP_DMAS = RES * 4
GN_EPS = 1e-5
W_SCALE = 64.0
LN_SCALE = 2.0 ** 40
LN2 = 0.6931471805599453
POOL_STEPS = 19
SETUP_READY = 15
WEIGHT_DMAS = 1 + 4 * RES
COL_DMAS = 2 + 2 * RES
X_STEPS = 10
Y_STEPS = 13


def at(sample, per, n):
    triple, offset = sample
    if triple is None:
        return offset * per + n
    return triple * (3 * per) + (offset * per + n)


def build(nc, x, g, w_qkv, mem_kv, w_out, b_out, w3, w1, b1, out):
    batch = x.shape[0]
    x_dram = x.rearrange("b (i r) h w -> b r i (h w)", r=RES)
    out_dram = out.rearrange("b (i r) h w -> b r i (h w)", r=RES)

    with ExitStack() as ctx:
        ctx.enter_context(nc.allow_low_precision(reason="bf16 carries only shifts of softmaxes and exact parts"))
        ctx.enter_context(nc.allow_non_contiguous_dma(reason="small weights in permuted order"))

        def sb(name, shape, dt=F32):
            return ctx.enter_context(nc.sbuf_tensor(name, shape, dt))

        def sem(name):
            return ctx.enter_context(nc.semaphore(name))

        conv_ps = ctx.enter_context(nc.psum_tensor("conv_ps", [P, 2, BANK], F32))
        sum_ps = ctx.enter_context(nc.psum_tensor("sum_ps", [P, BANK], F32))
        small_ps = ctx.enter_context(nc.psum_tensor("small_ps", [P, BANK], F32))
        pair_ps = [ctx.enter_context(nc.psum_tensor(f"pair{q}_ps", [P, UNIT], F32)) for q in range(2)]

        B = [sb(f"image{q}", [P, PIX]) for q in range(3)]
        U = sb("u", [P, PIX])
        KT = sb("exp_kT", [P, 2, UNIT])
        UB16 = KT[:].rearrange("p q n -> p (q n)").bitcast(BF16)
        SQ = KT
        UT = sb("uT", [P, 2, UB, P + 1])
        EQ = sb("exp_q", [P, PIX])
        YG = EQ
        HI = sb("yg_hi", [P, PAD, PAD], F16)
        LO = sb("yg_lo", [P, PAD, PAD], F16)
        REP = sb("replicas", [P, RES, PAD * PAD], F16)
        bn = sb("bn", [P, 2, CHUNKS, 6])
        st = sb("st", [P, 2, 16])
        nrm = sb("nrm", [P, BANK])
        den = sb("den", [P, BANK])
        part = sb("part", [P, BANK], BF16)
        R_norm = sb("r_norm", [P, BANK], BF16)
        R_den = sb("r_den", [P, BANK], BF16)
        km = sb("km", [P, 8])
        kneg_bf = sb("kneg_bf", [P, 2], BF16)
        kneg = sb("kneg", [P, 1])
        krow = sb("krow", [P, 4, P], BF16)
        pk = sb("pk", [P, MEM])
        pk_sum = sb("pk_sum", [P, 1])
        z = sb("z", [P, 2])
        qm = sb("qm", [P, P], BF16)
        qmT = sb("qmT", [P, P], BF16)
        A_sb = sb("a_sb", [P, P + MEM])
        AT_sb = sb("at_sb", [P, P])
        pkT_sb = sb("pkT_sb", [P, P])
        ctxT_sb = sb("ctxT_sb", [P, P])
        MT_sb = sb("mt_sb", [P, P])
        ident = sb("ident", [P, P])
        ident_bf = sb("ident_bf", [P, P], BF16)
        ones_bf = sb("ones_bf", [P, P], BF16)
        same_group = sb("same_group", [P, P])
        head_mask = sb("head_mask", [P, P])
        quad_mask = sb("quad_mask", [P, P])
        other_mask = sb("other_mask", [P, P])
        red_norm = sb("red_norm", [P, 2, 32])
        red_head = sb("red_head", [P, 2, 32])
        spread = sb("spread", [P, CHUNKS, P], BF16)
        minus_max = sb("minus_max", [P, BLOCKS, P], BF16)
        part_grid = sb("part_grid", [P, 4, 4, 8])
        part_mask = sb("part_mask", [P, 4])
        cut = sb("cut", [P, 2])
        mk = sb("mk", [P, MEM])
        mv = sb("mv", [P, MEM])
        mvT = sb("mvT", [P, P])
        wqkvT = sb("wqkvT", [P, 3, P])
        wqkT_bf = sb("wqkT_bf", [P, 2, P], BF16)
        woT = sb("woT", [P, P])
        gcol = sb("gcol", [P, 1])
        bo = sb("bo", [P, 1])
        b1s = sb("b1s", [P, 1])
        b01 = sb("b01", [P, 1])
        w_hi = sb("w_hi", [P, TAPS, P], F16)
        w_lo = sb("w_lo", [P, TAPS, P], F16)
        w_rep = sb("w_rep", [P, 2, 3, RES, 32], F16)
        w_mid = sb("w_mid", [P, 2, P], F16)
        idle = sb("idle", [P, 10])
        zcol = sb("zcol", [P, 3])

        raw_qkv = EQ[:, 0:3 * P].rearrange("p (t c) -> p t c", t=3)
        raw_out = EQ[:, 3 * P:4 * P]
        raw_b1 = EQ[:, 4 * P:5 * P]
        raw_w1 = EQ[:, 5 * P:6 * P]
        raw_w3 = EQ[:, 6 * P:15 * P]
        perm_qkv = B[2][:, 0:3 * P].rearrange("p (t r i) -> p t r i", t=3, r=RES)
        perm_w3 = B[2][:, 3 * P:12 * P].rearrange("p (t r i) -> p t r i", t=TAPS, r=RES)
        perm_w1 = B[2][:, 12 * P:13 * P].rearrange("p (r i) -> p r i", r=RES)
        tap32 = B[2][:, 13 * P:23 * P].rearrange("p (t c) -> p t c", t=TAPS + 1)

        x_in = [sem(f"x_in{q}") for q in range(3)]
        weights_in = sem("weights_in")
        stored = [sem(f"stored{u}") for u in range(UNITS)]
        rep_in = [sem(f"rep_in{h}") for h in range(2)]
        rep_weights_in = sem("rep_weights_in")
        col_in = sem("col_in")
        const_made = sem("const_made")
        setup_pe = sem("setup_pe")
        setup_dve = sem("setup_dve")
        x_stat = sem("x_stat")
        x_stat_act = sem("x_stat_act")
        x_group = sem("x_group")
        y_stat = sem("y_stat")
        y_stat_act = sem("y_stat_act")
        y_group = sem("y_group")
        xg_ready = sem("xg_ready")
        sq_ready = sem("sq_ready")
        norm_sum = sem("norm_sum")
        norm_dve = sem("norm_dve")
        norm_act = sem("norm_act")
        inv_bcast = sem("inv_bcast")
        u_ready = sem("u_ready")
        ub_ready = sem("ub_ready")
        k_rough = sem("k_rough")
        k_max = sem("k_max")
        q_rough = sem("q_rough")
        q_max = sem("q_max")
        max_turned = sem("max_turned")
        pk_ready = sem("pk_ready")
        kT_done = sem("kT_done")
        uT_done = sem("uT_done")
        kT_exp = sem("kT_exp")
        uT_kept = sem("uT_kept")
        ctx_sum = sem("ctx_sum")
        mix_dve = sem("mix_dve")
        mix_pe = sem("mix_pe")
        q_done = sem("q_done")
        q_exp = sem("q_exp")
        den_sum = sem("den_sum")
        den_act = sem("den_act")
        den_dve = sem("den_dve")
        den_bcast = sem("den_bcast")
        q_soft = sem("q_soft")
        mixed = sem("mixed")
        y_ready = sem("y_ready")
        yg_ready = sem("yg_ready")
        hi_ready = sem("hi_ready")
        lo_ready = sem("lo_ready")
        conv_done = sem("conv_done")
        out_ready = sem("out_ready")

        def px(t, v):
            return t[:, v * UNIT:(v + 1) * UNIT]

        def flat(t):
            return t[:].rearrange("p r c -> p (r c)")

        def inner(t, v):
            return t[:, 1 + v * UROWS:1 + (v + 1) * UROWS, 1:1 + SIDE]

        def rows(ap):
            return ap.rearrange("p (r c) -> p r c", c=SIDE)

        def first(sample):
            return sample[0] is None and sample[1] == 0

        def index(sample):
            triple, offset = sample
            return offset if triple is None else triple * 3 + offset

        def at_load(sample):
            triple, offset = sample
            loads = 16 * RES
            return loads * (offset // 3 + 1) if triple is None else triple * loads + loads * (offset // 3 + 1)

        def buffer_of(sample):
            return sample[1] % 3

        def image(sample):
            return B[buffer_of(sample)]

        def over_samples(eng, step):
            def known(s):
                return (None, s) if 0 <= s < batch else None

            def peeled(s):
                step(known(s), known(s - 1), known(s - 2), known(s + 1))

            for s in range(3):
                peeled(s)
            triples = (batch - 1) // 3
            with eng.Fori(1, triples) as t:
                for k in range(3):
                    step((t, k), (t, k - 1), (t, k - 2), (t, k + 1))
            for s in range(3 * triples, batch + 2):
                peeled(s)

        block = ctx.enter_context(nc.Block())

        @block.sync
        def _(sp):
            def load(s):
                for r in range(RES):
                    sp.dma_start(image(s)[32 * r:32 * r + 32], x_dram[index(s), r]).then_inc(x_in[buffer_of(s)], 16)

            def store(s, v):
                sp.wait_ge(out_ready, at(s, CHUNKS, 2 * v + 2))
                for r in range(RES):
                    sp.dma_start(out_dram[index(s), r][:, v * UNIT:(v + 1) * UNIT],
                                 px(image(s), v)[32 * r:32 * r + 32]).then_inc(stored[v], 16)

            def replicate(s, half, e=None):
                first_col, end_col = (0, SPLIT * PAD - 2) if half == 0 else (SPLIT * PAD, PAD * PAD - 2)
                sp.wait_ge(lo_ready, at(s, UNITS, 3 + half))
                if e is not None:
                    sp.wait_ge(conv_done, at(e, CHUNKS, CHUNKS))
                for r in range(RES):
                    q = slice(32 * r, 32 * r + 32)
                    for shift in range(3):
                        sp.dma_start(REP[32 * shift:32 * shift + 32, r, first_col:end_col],
                                     flat(HI)[q, first_col + shift:end_col + shift]).then_inc(rep_in[half], 16)
                    sp.dma_start(REP[96:128, r, first_col:end_col],
                                 flat(LO)[q, first_col:end_col]).then_inc(rep_in[half], 16)

            load((None, 0))
            sp.dma_start(raw_qkv, w_qkv.rearrange("(t o) c -> o t c", t=3)).then_inc(weights_in, 16)
            n = 1
            for r in range(RES):
                q = slice(32 * r, 32 * r + 32)
                sp.dma_start(raw_w3[q], w3.rearrange("(i r) c a b -> r i (c a b)", r=RES)[r]).then_inc(weights_in, 16)
                sp.dma_start(raw_w1[q], w1.rearrange("(i r) c -> r i c", r=RES)[r]).then_inc(weights_in, 16)
                sp.dma_start(raw_b1[q], b1.rearrange("(i r) c -> r i c", r=RES)[r]).then_inc(weights_in, 16)
                sp.dma_start(raw_out[q], w_out.rearrange("(i r) c -> r i c", r=RES)[r]).then_inc(weights_in, 16)
                n += 4
            assert n == WEIGHT_DMAS

            def step(a, c, e, p):
                if e is not None:
                    store(e, 2)
                    store(e, 3)
                if p is not None:
                    if e is not None:
                        for v in range(UNITS):
                            sp.wait_ge(stored[v], at(e, 16 * RES, 16 * RES))
                    elif a[1] == 1:
                        sp.wait_ge(setup_dve, SETUP_READY)
                    load(p)
                if c is not None:
                    replicate(c, 0, e)
                    replicate(c, 1)
                    store(c, 0)
                    store(c, 1)

            over_samples(sp, step)
            for v in range(UNITS):
                sp.wait_ge(stored[v], 16 * RES * batch)

        @block.gpsimd
        def _(pool):
            made = 0

            def make(ins):
                nonlocal made
                ins.then_inc(const_made, 1)
                made += 1
                pool.wait_ge(const_made, made)

            n = 0
            for r in range(RES):
                q = slice(32 * r, 32 * r + 32)
                pool.dma_start(gcol[q], g.rearrange("(i r one) -> r i one", r=RES, one=1)[r]).then_inc(col_in, 16)
                pool.dma_start(bo[q], b_out.rearrange("(i r one) -> r i one", r=RES, one=1)[r]).then_inc(col_in, 16)
                n += 2
            pool.dma_start(mk[:], mem_kv[0].rearrange("h d j -> (h d) j")).then_inc(col_in, 16)
            pool.dma_start(mv[:], mem_kv[1].rearrange("h d j -> (h d) j")).then_inc(col_in, 16)
            assert n + 2 == COL_DMAS
            make(pool.memset(ident[:], 0.0))
            make(pool.affine_select(out=ident[:], in_=ident[:], compare_op=ALU.not_equal, fill=1.0, base=0,
                                    pattern=[[-1, P]], channel_multiplier=1))
            make(pool.tensor_copy(ident_bf[:], ident[:]))
            make(pool.memset(same_group[:], 0.0))
            for k in range(-(RES - 1), RES):
                make(pool.affine_select(out=same_group[:], in_=same_group[:], compare_op=ALU.not_equal,
                                        fill=1.0 / RES, base=32 * k, pattern=[[-1, P]], channel_multiplier=1))
            make(pool.memset(spread[:], 0.0))
            for part_no in range(3):
                make(pool.affine_select(out=spread[:], in_=spread[:], compare_op=ALU.not_equal, fill=1.0,
                                        base=-8 * part_no, pattern=[[-4, 2], [-32, 4], [-1, HEADS], [0, DH]],
                                        channel_multiplier=1))
            make(pool.memset(minus_max[:], 0.0))
            make(pool.affine_select(out=minus_max[:], in_=minus_max[:], compare_op=ALU.not_equal, fill=-1.0,
                                    base=0, pattern=[[-4, BLOCKS], [-1, HEADS], [0, DH]], channel_multiplier=1))
            make(pool.memset(part_grid[:], 0.0))
            make(pool.affine_select(out=part_grid[:], in_=part_grid[:], compare_op=ALU.not_equal, fill=1.0,
                                    base=0, pattern=[[-8, 4], [-32, 4], [-1, 8]], channel_multiplier=1))
            assert made == POOL_STEPS
            make(pool.memset(idle[:, 3:4], 0.0))

            def take_wait(column):
                pool.tensor_tensor(idle[:, column:column + 1], idle[:, 3:4], idle[:, 3:4], ALU.add)

            def group_norm_x(a, p):
                pool.wait_ge(x_stat, at(p, X_STEPS, X_STEPS))
                take_wait(5)
                for v in range(UNITS):
                    if a is not None:
                        pool.wait_ge(q_done, at(a, UNITS, v + 1))
                        take_wait(6 + v)
                    pool.tensor_scalar(px(U, v), px(image(p), v), st[:, 0, 9:10],
                                       st[:, 0, 10:11], ALU.mult, ALU.add).then_inc(xg_ready, 1)

            def step(a, c, e, p):
                if c is not None:
                    pool.wait_ge(y_stat, at(c, Y_STEPS, Y_STEPS))
                    take_wait(4)
                    for v in range(UNITS):
                        pool.tensor_scalar(px(YG, v), px(image(c), v), st[:, 1, 9:10], st[:, 1, 11:12],
                                           ALU.mult, ALU.add).then_inc(yg_ready, 1)
                if p is not None:
                    group_norm_x(a, p)

            group_norm_x(None, (None, 0))
            over_samples(pool, step)

        @block.scalar
        def _(act):
            act.wait_ge(setup_dve, SETUP_READY)

            def stat_act(s, per, dve, mine, slot):
                act.wait_ge(dve, at(s, per, 6 if per == X_STEPS else 7))
                act.activation(st[:, slot, 6:7], st[:, slot, 5:6], ACT.Ln, bias=zcol[:, 0:1]).then_inc(mine, 1)
                act.wait_ge(mine, at(s, 2, 1))
                act.activation(st[:, slot, 7:8], st[:, slot, 6:7], ACT.Exp, scale=-0.5,
                               bias=zcol[:, 0:1]).then_inc(mine, 1)

            def square(p, v):
                act.wait_ge(xg_ready, at(p, UNITS, v + 1))
                if v >= 2:
                    act.wait_ge(norm_sum, at(p, UNITS, v - 1))
                act.activation(SQ[:, v % 2], px(U, v), ACT.Square, bias=zcol[:, 0:1]).then_inc(sq_ready, 1)

            def inverse_norm(p):
                act.wait_ge(norm_dve, at(p, 5, 1))
                act.activation(nrm[:], nrm[:], ACT.Ln, scale=LN_SCALE, bias=zcol[:, 0:1]).then_inc(norm_act, 1)
                act.wait_ge(norm_act, at(p, 2, 1))
                act.activation(nrm[:], nrm[:], ACT.Exp, scale=-0.5, bias=zcol[:, 1:2]).then_inc(norm_act, 1)

            def high_part(c, e, v):
                if v == 0:
                    act.wait_ge(y_stat, at(c, Y_STEPS, Y_STEPS))
                    if e is not None:
                        act.wait_ge(conv_done, at(e, CHUNKS, CHUNKS))
                act.activation(inner(HI, v), rows(px(image(c), v)), ACT.Identity, scale=st[:, 1, 9:10],
                               bias=st[:, 1, 11:12]).then_inc(hi_ready, 1)

            def step(a, c, e, p):
                if a is not None:
                    for v in range(UNITS):
                        act.wait_ge(u_ready, at(a, UNITS, v + 1))
                        act.activation(px(UB16, v), px(U, v), ACT.Copy).then_inc(ub_ready, 1)
                if a is not None:
                    act.wait_ge(k_max, at(a, 8, 7))
                    act.activation(pk[:], mk[:], ACT.Exp, bias=kneg[:], accum_out=pk_sum[:]).then_inc(pk_ready, 1)
                for v in range(UNITS):
                    if c is not None and v == 1:
                        stat_act(c, Y_STEPS, y_stat, y_stat_act, 1)
                    if c is not None and v >= 2:
                        high_part(c, e, 2 * v - 4)
                        high_part(c, e, 2 * v - 3)
                    if a is not None:
                        act.wait_ge(kT_done, at(a, UNITS, v + 1))
                        if v >= 2:
                            act.wait_ge(ctx_sum, at(a, UNITS, v - 1))
                        act.activation(KT[:, v % 2], pair_ps[0][:], ACT.Exp, bias=zcol[:, 0:1]).then_inc(kT_exp, 1)
                        act.wait_ge(uT_done, at(a, UNITS, v + 1))
                        act.activation(UT[:, v % 2, :, 0:P], pair_ps[1][:].rearrange("p (b c) -> p b c", c=P),
                                       ACT.Copy).then_inc(uT_kept, 1)
                if a is not None:
                    for v in range(UNITS):
                        if v == 2 and p is not None:
                            stat_act(p, X_STEPS, x_stat, x_stat_act, 0)
                        act.wait_ge(q_done, at(a, UNITS, v + 1))
                        if c is not None:
                            act.wait_ge(lo_ready, at(c, UNITS, v + 1))
                        act.activation(px(EQ, v), pair_ps[v % 2][:], ACT.Exp, bias=zcol[:, 0:1]).then_inc(q_exp, 1)
                    act.wait_ge(den_sum, at(a, 1, 1))
                    act.activation(den[:], sum_ps[:], ACT.Ln, bias=zcol[:, 0:1]).then_inc(den_act, 1)
                    act.wait_ge(den_act, at(a, 2, 1))
                    act.activation(den[:], den[:], ACT.Exp, scale=-1.0, bias=zcol[:, 0:1]).then_inc(den_act, 1)
                if p is not None:
                    for v in range(UNITS):
                        square(p, v)
                    inverse_norm(p)

            stat_act((None, 0), X_STEPS, x_stat, x_stat_act, 0)
            for v in range(UNITS):
                square((None, 0), v)
            inverse_norm((None, 0))
            for q in range(4):
                for r in range(RES):
                    c = slice(32 * r, 32 * r + 32)
                    for part, w in enumerate((w_hi, w_lo)):
                        act.dma_start(w_rep[32 * q:32 * q + 32, part, :, r, :],
                                      w[c].rearrange("p (dy dx) o -> p dy dx o", dx=3)[:, :, q % 3, c]
                                      ).then_inc(rep_weights_in, 16)
            over_samples(act, step)

        @block.tensor
        def _(pe):
            pe.wait_ge(const_made, POOL_STEPS)
            pe.wait_ge(col_in, 16 * COL_DMAS)
            pe.wait_ge(setup_dve, 3)
            def turn(dst, src, m=P):
                return pe.transpose(dst, src, ident[:])
            for t in range(3):
                turn(conv_ps[:, 0, t * P:(t + 1) * P], perm_qkv[:, t].rearrange("p r i -> p (r i)"))
            turn(conv_ps[:, 0, 3 * P:4 * P], raw_out)
            pe.transpose(small_ps[0:MEM, 0:P], mv[:], ident[:])
            for t in range(TAPS + 1):
                src = perm_w3[:, t] if t < TAPS else perm_w1
                bank = [pair_ps[0][:, 0:BANK], pair_ps[0][:, BANK:UNIT], pair_ps[1][:, 0:BANK]][t // 4]
                last = turn(bank[:, (t % 4) * P:(t % 4 + 1) * P], src.rearrange("p r i -> p (r i)"))
            last.then_inc(setup_pe, 1)
            pe.wait_ge(setup_dve, SETUP_READY)

            def norm_sums(p, v):
                pe.wait_ge(sq_ready, at(p, UNITS, v + 1))
                for j in (2 * v, 2 * v + 1):
                    t, s = j % 4, j // 4
                    mm = pe.matmul(sum_ps[32 * t:32 * t + 32, :], red_norm[:, s], SQ[:, v % 2, (j % 2) * BANK:(j % 2 + 1) * BANK],
                                   start=(s == 0), stop=(s == 1))
                mm.then_inc(norm_sum, 1)

            def broadcast(R, v, done):
                for j in (2 * v, 2 * v + 1):
                    mm = pe.matmul(pair_ps[v % 2][:, (j % 2) * BANK:(j % 2 + 1) * BANK], spread[:, j], R[:],
                                   start=True, stop=True)
                mm.then_inc(done, 1)

            def inv_norm(a, c, v):
                if v == 0:
                    pe.wait_ge(norm_dve, at(a, 5, 5))
                if v < 2 and c is not None:
                    pe.wait_ge(y_ready, at(c, UNITS, 3 + v))
                if v >= 2:
                    pe.wait_ge(u_ready, at(a, UNITS, v - 1))
                broadcast(R_norm, v, inv_bcast)

            def rough_k(a, v):
                pe.wait_ge(ub_ready, at(a, UNITS, v + 1))
                if v < 2:
                    pe.wait_ge(u_ready, at(a, UNITS, v + 3))
                else:
                    pe.wait_ge(k_max, at(a, 8, v - 1))
                for j in (2 * v, 2 * v + 1):
                    mm = pe.matmul(pair_ps[v % 2][:, (j % 2) * BANK:(j % 2 + 1) * BANK], wqkT_bf[:, 1],
                                   UB16[:, j * BANK:(j + 1) * BANK], start=True, stop=True)
                mm.then_inc(k_rough, 1)

            def rough_q(a, v):
                if v < 2:
                    pe.wait_ge(k_max, at(a, 8, v + 3))
                else:
                    pe.wait_ge(q_max, at(a, 5, v - 1))
                for b in range(UB):
                    c0 = (v * UB + b) * P
                    mm = pe.matmul(pair_ps[v % 2][:, b * P:(b + 1) * P], UB16[:, c0:c0 + P], wqkT_bf[:, 0],
                                   start=True, stop=True)
                mm.then_inc(q_rough, 1)

            def keys(a, v):
                if v == 0:
                    pe.wait_ge(k_max, at(a, 8, 8))
                    pe.wait_ge(q_max, at(a, 5, 3))
                else:
                    pe.wait_ge(kT_exp, at(a, UNITS, v))
                for half in range(2):
                    bank = pair_ps[0][:, half * BANK:(half + 1) * BANK]
                    pe.matmul(bank, ones_bf[:], krow[:].rearrange("p a b -> p (a b)"), start=True, stop=False,
                              skip_group_check=True)
                    for b in range(4):
                        c0 = (v * UB + half * 4 + b) * P
                        mm = pe.matmul(bank[:, b * P:(b + 1) * P], U[:, c0:c0 + P], wqkvT[:, 1],
                                       start=False, stop=(b == 3), skip_group_check=True)
                mm.then_inc(kT_done, 1)

            def turn_u(a, v):
                if v == 0:
                    pe.wait_ge(q_max, at(a, 5, 4))
                else:
                    pe.wait_ge(uT_kept, at(a, UNITS, v))
                for b in range(UB):
                    c0 = (v * UB + b) * P
                    mm = pe.transpose(pair_ps[1][:, b * P:(b + 1) * P], U[:, c0:c0 + P], ident[:])
                mm.then_inc(uT_done, 1)

            def context(a, v):
                pe.wait_ge(kT_exp, at(a, UNITS, v + 1))
                pe.wait_ge(uT_kept, at(a, UNITS, v + 1))
                for b in range(UB):
                    mm = pe.matmul(sum_ps[:, 0:P + 1], KT[:, v % 2, b * P:(b + 1) * P], UT[:, v % 2, b],
                                   start=(v == 0 and b == 0), stop=(v == UNITS - 1 and b == UB - 1))
                mm.then_inc(ctx_sum, 1)

            def queries(a, v):
                if v == 0:
                    pe.wait_ge(q_max, at(a, 5, 5))
                    pe.wait_ge(kT_exp, at(a, UNITS, UNITS))
                elif v == 1:
                    pe.wait_ge(uT_kept, at(a, UNITS, UNITS))
                else:
                    pe.wait_ge(q_exp, at(a, UNITS, v - 1))
                for j in (2 * v, 2 * v + 1):
                    bank = pair_ps[v % 2][:, (j % 2) * BANK:(j % 2 + 1) * BANK]
                    pe.matmul(bank, wqkvT[:, 0], U[:, j * BANK:(j + 1) * BANK], start=True, stop=False,
                              skip_group_check=True)
                    for b in range(4):
                        mm = pe.matmul(bank[:, b * P:(b + 1) * P], minus_max[:, 4 * j + b], qmT[:],
                                       start=False, stop=(b == 3), skip_group_check=True)
                mm.then_inc(q_done, 1)

            def denominators(a):
                pe.wait_ge(mix_dve, at(a, 8, 3))
                for j in range(CHUNKS):
                    t, s = j % 4, j // 4
                    if j % 2 == 0:
                        pe.wait_ge(q_exp, at(a, UNITS, j // 2 + 1))
                    mm = pe.matmul(sum_ps[32 * t:32 * t + 32, :], red_head[:, s], EQ[:, j * BANK:(j + 1) * BANK],
                                   start=(s == 0), stop=(s == 1))
                mm.then_inc(den_sum, 1)

            def den_broadcast(a, v):
                if v < 2:
                    if v == 0:
                        pe.wait_ge(den_dve, at(a, 4, 4))
                    pe.wait_ge(q_exp, at(a, UNITS, v + 3))
                else:
                    pe.wait_ge(y_ready, at(a, UNITS, v - 1))
                broadcast(R_den, v, den_bcast)

            def mix(a, v):
                if v == 0:
                    pe.wait_ge(mix_dve, at(a, 8, 8))
                pe.wait_ge(q_soft, at(a, UNITS, v + 1))
                for j in (2 * v, 2 * v + 1):
                    mm = pe.matmul(pair_ps[v % 2][:, (j % 2) * BANK:(j % 2 + 1) * BANK], MT_sb[:],
                                   EQ[:, j * BANK:(j + 1) * BANK], start=True, stop=True)
                mm.then_inc(mixed, 1)

            def conv_dense(s, j):
                if s is None:
                    return
                if j % 4 == 0:
                    pe.wait_ge(rep_in[j // 4], at(s, 16 * REP_DMAS, 16 * REP_DMAS))
                if j >= 2 or not first(s):
                    pe.wait_ge(out_ready, at(s, CHUNKS, max(0, j - 1)))
                whole = [(w_mid[:, part], HI, 1, 1) for part in range(2)]
                whole += [(w_hi[:, 3 * dy + dx], LO, dy, dx) for dy in range(3) for dx in (1, 2)]
                for n, (w, data, dy, dx) in enumerate(whole):
                    pe.matmul(conv_ps[:, j % 2], w, data[:, j * ROWS + dy:(j + 1) * ROWS + dy, dx:dx + SIDE],
                              start=(n == 0), stop=False, skip_group_check=True)

            def conv_replicas(s, j):
                if s is None:
                    return
                if first(s) and j == 0:
                    pe.wait_ge(rep_weights_in, 16 * 8 * RES)
                for dy in range(3):
                    for part in range(2):
                        for r in range(RES):
                            rep = REP[:, r].rearrange("p (y x) -> p y x", x=PAD)
                            mm = pe.matmul(conv_ps[32 * r:32 * r + 32, j % 2], w_rep[:, part, dy, r],
                                           rep[:, j * ROWS + dy:(j + 1) * ROWS + dy, 0:SIDE],
                                           start=False, stop=(dy == 2 and part == 1), skip_group_check=True)
                mm.then_inc(conv_done, 1)

            def group_means(src, done):
                pe.matmul(small_ps[:, 0:2], same_group[:], st[:, src, 0:2], start=True, stop=True).then_inc(done, 1)

            def turn_k_max(a, c):
                if c is not None:
                    pe.wait_ge(mix_dve, at(c, 8, 8))
                pe.wait_ge(k_max, at(a, 8, 6))
                pe.transpose(small_ps[0:1, 0:P // 2].bitcast(BF16), kneg_bf[:, 0:1], ident_bf[:]).then_inc(max_turned, 1)

            def turn_q_max(a):
                pe.wait_ge(k_max, at(a, 8, 8))
                pe.wait_ge(q_max, at(a, 5, 4))
                pe.transpose(small_ps[:, 0:P // 2].bitcast(BF16), qm[:], ident_bf[:]).then_inc(max_turned, 1)

            def y_means(a, c):
                if a is not None:
                    pe.wait_ge(q_max, at(a, 5, 5))
                else:
                    pe.wait_ge(mix_dve, at(c, 8, 8))
                pe.wait_ge(y_stat, at(c, Y_STEPS, 4))
                group_means(1, y_group)

            def step(a, c, e, p):
                if a is not None:
                    inv_norm(a, c, 0)
                    inv_norm(a, c, 1)
                conv_dense(e, 4)
                if a is not None:
                    inv_norm(a, c, 2)
                conv_replicas(e, 4)
                if a is not None:
                    inv_norm(a, c, 3)
                conv_dense(e, 5)
                if a is not None:
                    rough_k(a, 0)
                    rough_k(a, 1)
                conv_replicas(e, 5)
                if a is not None:
                    rough_k(a, 2)
                conv_dense(e, 6)
                if a is not None:
                    rough_k(a, 3)
                conv_replicas(e, 6)
                if a is not None:
                    rough_q(a, 0)
                conv_dense(e, 7)
                if a is not None:
                    rough_q(a, 1)
                    turn_k_max(a, c)
                    rough_q(a, 2)
                conv_replicas(e, 7)
                if a is not None:
                    rough_q(a, 3)
                    for v in range(UNITS):
                        keys(a, v)
                        if v == 0:
                            turn_q_max(a)
                        turn_u(a, v)
                        if v == 0:
                            if c is not None:
                                y_means(a, c)
                        else:
                            context(a, v - 1)
                    queries(a, 0)
                    context(a, 3)
                    queries(a, 1)
                if p is not None:
                    pe.wait_ge(x_stat, at(p, X_STEPS, 3))
                    if c is not None:
                        pe.wait_ge(y_stat, at(c, Y_STEPS, 5))
                    else:
                        pe.wait_ge(q_max, at(a, 5, 5))
                    group_means(0, x_group)
                if a is not None:
                    queries(a, 2)
                    pe.wait_ge(mix_dve, at(a, 8, 4))
                    if p is not None:
                        pe.wait_ge(x_stat, at(p, X_STEPS, 4))
                    elif c is not None:
                        pe.wait_ge(y_stat, at(c, Y_STEPS, 5))
                    pe.transpose(small_ps[:, 0:P], A_sb[:, 0:P], ident[:])
                    pe.transpose(small_ps[0:MEM, P:2 * P], A_sb[:, P:P + MEM], ident[:]).then_inc(mix_pe, 1)
                    queries(a, 3)
                    pe.wait_ge(mix_dve, at(a, 8, 6))
                    pe.matmul(small_ps[:, 0:P], wqkvT[:, 2], AT_sb[:], start=True, stop=False)
                    pe.matmul(small_ps[:, 0:P], mvT[0:MEM], pkT_sb[0:MEM], start=False, stop=True).then_inc(mix_pe, 1)
                    denominators(a)
                if a is None and c is not None:
                    y_means(a, c)
                conv_dense(c, 0)
                conv_replicas(c, 0)
                if a is not None:
                    pe.wait_ge(mix_dve, at(a, 8, 7))
                    pe.matmul(small_ps[:, 0:P], ctxT_sb[:], woT[:], start=True, stop=True).then_inc(mix_pe, 1)
                conv_dense(c, 1)
                if p is not None:
                    pe.wait_ge(den_act, at(a, 2, 1))
                    norm_sums(p, 0)
                    norm_sums(p, 1)
                conv_replicas(c, 1)
                if a is not None:
                    den_broadcast(a, 0)
                    den_broadcast(a, 1)
                conv_dense(c, 2)
                if p is not None:
                    norm_sums(p, 2)
                    norm_sums(p, 3)
                if a is not None:
                    mix(a, 0)
                    mix(a, 1)
                conv_replicas(c, 2)
                if a is not None:
                    den_broadcast(a, 2)
                    den_broadcast(a, 3)
                conv_dense(c, 3)
                if a is not None:
                    mix(a, 2)
                    mix(a, 3)
                conv_replicas(c, 3)

            pe.wait_ge(x_stat, 3)
            group_means(0, x_group)
            for v in range(UNITS):
                norm_sums((None, 0), v)
            over_samples(pe, step)

        @block.vector
        def _(dve):
            made = 0

            def make(ins, wait=False):
                nonlocal made
                ins.then_inc(setup_dve, 1)
                made += 1
                if wait:
                    dve.wait_ge(setup_dve, made)

            dve.wait_ge(weights_in, 16 * WEIGHT_DMAS)
            make(dve.tensor_copy(perm_qkv, raw_qkv.rearrange("p t (i r) -> p t r i", r=RES)))
            make(dve.tensor_copy(perm_w1, raw_w1.rearrange("p (i r) -> p r i", r=RES)))
            for t in range(TAPS):
                last = dve.tensor_copy(perm_w3[:, t], raw_w3.rearrange("p (i r t) -> p t r i", r=RES, t=TAPS)[:, t])
            make(last)
            for t in (ones_bf, UT):
                dve.memset(t[:], 1.0)
            for t in (HI, LO, krow, head_mask, quad_mask, red_norm, red_head):
                last = dve.memset(t[:], 0.0)
            make(last, wait=True)
            dve.memset(other_mask[:], 1.0)
            for h in range(HEADS):
                q = slice(DH * h, DH * h + DH)
                dve.memset(head_mask[q, q], DH ** -0.5)
                dve.memset(quad_mask[q, q], 1.0)
            for s in range(2):
                dve.memset(red_norm[:, s].rearrange("p (part s h) -> p part s h", s=2, h=4)[:, :, s, :], 1.0)
                for h in range(HEADS):
                    q = slice(DH * h, DH * h + DH)
                    dve.memset(red_head[q, s].rearrange("p (part s h) -> p part s h", s=2, h=4)[:, :, s, h:h + 1], 1.0)
            dve.memset(zcol[:, 0:1], 0.0)
            dve.memset(zcol[:, 1:2], 0.5 * (7 + 40) * LN2)
            last = dve.tensor_reduce(b1s[:], raw_b1, AX.X, ALU.add)
            make(last, wait=True)
            for h in range(HEADS):
                q = slice(DH * h, DH * h + DH)
                last = dve.memset(other_mask[q, q], 0.0)
            make(last, wait=True)
            dve.wait_ge(const_made, POOL_STEPS)
            make(dve.tensor_reduce(part_mask[:], part_grid[:].rearrange("p k t w -> p k (t w)"), AX.X, ALU.add), wait=True)
            dve.tensor_scalar(cut[:, 0:1], part_mask[:, 0:1], -1.0, None, ALU.add)
            dve.tensor_scalar(cut[:, 1:2], part_mask[:, 2:3], -1.0, None, ALU.mult)
            dve.wait_ge(col_in, 16 * COL_DMAS)
            dve.tensor_tensor(b01[:], bo[:], b1s[:], ALU.add)
            make(dve.tensor_reduce(km[:, 4:5], mk[:], AX.X, ALU.max))
            dve.wait_ge(setup_pe, 1)
            make(dve.tensor_scalar(wqkvT[:].rearrange("p t c -> p (t c)"), conv_ps[:, 0, 0:3 * P], gcol[:], None,
                                   ALU.mult), wait=True)
            dve.tensor_copy(wqkT_bf[:], wqkvT[:, 0:2])
            dve.tensor_copy(woT[:], conv_ps[:, 0, 3 * P:4 * P])
            dve.tensor_copy(mvT[0:MEM], small_ps[0:MEM, 0:P])
            for t in range(TAPS + 1):
                bank = [pair_ps[0][:, 0:BANK], pair_ps[0][:, BANK:UNIT], pair_ps[1][:, 0:BANK]][t // 4]
                last = dve.scalar_tensor_tensor(out=tap32[:, t], in0=bank[:, (t % 4) * P:(t % 4 + 1) * P], scalar=W_SCALE,
                                                in1=quad_mask[:] if t < TAPS else other_mask[:],
                                                op0=ALU.mult, op1=ALU.mult)
            make(last, wait=True)
            make(dve.tensor_tensor(tap32[:, TAPS // 2], tap32[:, TAPS // 2], tap32[:, TAPS], ALU.add), wait=True)
            make(dve.tensor_copy(w_hi[:], tap32[:, 0:TAPS]), wait=True)
            make(dve.tensor_tensor(w_lo[:], tap32[:, 0:TAPS], w_hi[:], ALU.subtract), wait=True)
            make(dve.tensor_copy(w_mid[:, 0], tap32[:, TAPS]), wait=True)
            make(dve.tensor_tensor(w_mid[:, 1], tap32[:, TAPS], w_mid[:, 0], ALU.subtract), wait=True)
            assert made == SETUP_READY, made

            def chain(sem_, sample, per, n):
                def did(ins, wait=True):
                    nonlocal n
                    ins.then_inc(sem_, 1)
                    n += 1
                    if wait:
                        dve.wait_ge(sem_, at(sample, per, n))
                return did

            def channel_stats(slot, did):
                dve.memset(idle[:, 2:3], 0.0)
                did(dve.bn_aggr(st[:, slot, 0:2], bn[:, slot].rearrange("p c s -> p (c s)")))
                if slot == 1:
                    did(dve.tensor_tensor(st[:, slot, 0:1], st[:, slot, 0:1], b1s[:], ALU.subtract))
                did(dve.scalar_tensor_tensor(out=st[:, slot, 1:2], in0=st[:, slot, 0:1], scalar=st[:, slot, 0:1],
                                             in1=st[:, slot, 1:2], op0=ALU.mult, op1=ALU.add), wait=False)

            def variance(slot, did):
                did(dve.tensor_copy(st[:, slot, 2:4], small_ps[:, 0:2]))
                did(dve.scalar_tensor_tensor(out=st[:, slot, 4:5], in0=st[:, slot, 2:3], scalar=st[:, slot, 2:3],
                                             in1=st[:, slot, 3:4], op0=ALU.mult, op1=ALU.subtract))
                did(dve.tensor_scalar(st[:, slot, 5:6], st[:, slot, 4:5], -1.0, GN_EPS, ALU.mult, ALU.add), wait=False)

            def scale_shift(slot, did):
                did(dve.scalar_tensor_tensor(out=st[:, slot, 8:9], in0=st[:, slot, 7:8], scalar=st[:, slot, 7:8],
                                             in1=st[:, slot, 5:6], op0=ALU.mult, op1=ALU.mult))
                did(dve.tensor_scalar(st[:, slot, 8:9], st[:, slot, 8:9], -0.5, 1.5, ALU.mult, ALU.add))
                did(dve.tensor_tensor(st[:, slot, 9:10], st[:, slot, 8:9], st[:, slot, 7:8], ALU.mult))
                did(dve.tensor_scalar(st[:, slot, 10:11], st[:, slot, 2:3], st[:, slot, 9:10], -1.0,
                                      ALU.mult, ALU.mult), wait=(slot == 1))
                if slot == 1:
                    did(dve.tensor_scalar(st[:, slot, 12:13], b1s[:], st[:, slot, 9:10], -1.0, ALU.mult, ALU.mult))
                    did(dve.tensor_tensor(st[:, slot, 11:12], st[:, slot, 12:13], st[:, slot, 10:11], ALU.add), wait=False)

            def x_stats(p, first):
                if first:
                    dve.wait_ge(x_in[buffer_of(p)], at_load(p))
                for j in range(0 if first else 4, 4 if first else CHUNKS):
                    last = dve.bn_stats(bn[:, 0, j], image(p)[:, j * BANK:(j + 1) * BANK])
                if not first:
                    did = chain(x_stat, p, X_STEPS, 0)
                    did(last)
                    channel_stats(0, did)

            def x_variance(p):
                dve.wait_ge(x_group, at(p, 1, 1))
                variance(0, chain(x_stat, p, X_STEPS, 3))

            def x_scale(p):
                dve.wait_ge(x_stat_act, at(p, 2, 2))
                scale_shift(0, chain(x_stat, p, X_STEPS, 6))

            def three_parts(src, R, did):
                did(dve.tensor_copy(part[:], src[:]))
                did(dve.scalar_tensor_tensor(out=src[:], in0=part[:], scalar=cut[:, 0:1], in1=src[:],
                                             op0=ALU.mult, op1=ALU.add))
                did(dve.tensor_copy(part[:], src[:]))
                did(dve.scalar_tensor_tensor(out=R[:], in0=part[:], scalar=cut[:, 1:2], in1=src[:],
                                             op0=ALU.mult, op1=ALU.add), wait=False)

            def norm_guard(p):
                dve.wait_ge(norm_sum, at(p, UNITS, UNITS))
                dve.tensor_scalar(nrm[:], sum_ps[:], 1e-24, None, ALU.max).then_inc(norm_dve, 1)

            def norm_parts(p):
                dve.wait_ge(norm_act, at(p, 2, 2))
                three_parts(nrm, R_norm, chain(norm_dve, p, 5, 1))

            def normalise(a, v):
                dve.wait_ge(inv_bcast, at(a, UNITS, v + 1))
                dve.tensor_tensor(px(U, v), px(U, v), pair_ps[v % 2][:], ALU.mult).then_inc(u_ready, 1)

            def low_part(c, v):
                dve.wait_ge(yg_ready, at(c, UNITS, v + 1))
                dve.wait_ge(hi_ready, at(c, UNITS, v + 1))
                dve.tensor_tensor(inner(LO, v), rows(px(YG, v)), inner(HI, v), ALU.subtract).then_inc(lo_ready, 1)

            def max_k(a, v):
                dve.wait_ge(k_rough, at(a, UNITS, v + 1))
                dve.tensor_reduce(km[:, v:v + 1], pair_ps[v % 2][:], AX.X, ALU.max).then_inc(k_max, 1)

            def max_q(a, v):
                dve.wait_ge(q_rough, at(a, UNITS, v + 1))
                dve.tensor_reduce(qm[:, v * 32:(v + 1) * 32], pair_ps[v % 2][:].rearrange("p (b d) -> p b d", d=DH),
                                  AX.X, ALU.max).then_inc(q_max, 1)

            def finish(s, j):
                if s is None:
                    return
                chunk = image(s)[:, j * BANK:(j + 1) * BANK]
                dve.wait_ge(conv_done, at(s, CHUNKS, j + 1))
                dve.scalar_tensor_tensor(out=chunk, in0=conv_ps[:, j % 2], scalar=1.0 / W_SCALE, in1=chunk,
                                         op0=ALU.mult, op1=ALU.add).then_inc(out_ready, 1)

            def soften(a, v):
                dve.wait_ge(den_bcast, at(a, UNITS, v + 1))
                dve.tensor_tensor(px(EQ, v), px(EQ, v), pair_ps[v % 2][:], ALU.mult).then_inc(q_soft, 1)

            def residual(a, v):
                dve.wait_ge(mixed, at(a, UNITS, v + 1))
                unit = px(image(a), v)
                dve.scalar_tensor_tensor(out=unit, in0=pair_ps[v % 2][:], scalar=b01[:], in1=unit,
                                         op0=ALU.add, op1=ALU.add).then_inc(y_ready, 1)

            def y_bn(a, v):
                if a is None:
                    return
                dve.wait_ge(y_ready, at(a, UNITS, v + 1))
                for j in (2 * v, 2 * v + 1):
                    last = dve.bn_stats(bn[:, 1, j], image(a)[:, j * BANK:(j + 1) * BANK])
                return last

            def step(a, c, e, p):
                if a is not None:
                    normalise(a, 0)
                    normalise(a, 1)
                    normalise(a, 2)
                finish(e, 4)
                if a is not None:
                    normalise(a, 3)
                y_bn(c, 0)
                if a is not None:
                    max_k(a, 0)
                    max_k(a, 1)
                finish(e, 5)
                y_bn(c, 1)
                if a is not None:
                    max_k(a, 2)
                    max_k(a, 3)
                    did = chain(k_max, a, 8, 4)
                    dve.wait_ge(k_max, at(a, 8, 4))
                    did(dve.tensor_reduce(km[:, 5:6], km[:, 0:5], AX.X, ALU.max))
                    did(dve.tensor_scalar(kneg_bf[:, 0:1], km[:, 5:6], -1.0, None, ALU.mult))
                    did(dve.tensor_copy(kneg[:], kneg_bf[:, 0:1]), wait=False)
                finish(e, 6)
                y_bn(c, 2)
                if a is not None:
                    max_q(a, 0)
                    max_q(a, 1)
                    dve.wait_ge(max_turned, at(a, 2, 1))
                    dve.tensor_copy(krow[0:1], small_ps[0:1, 0:P // 2].bitcast(BF16).unsqueeze(1).to_broadcast([1, 4, P])
                                    ).then_inc(k_max, 1)
                    max_q(a, 2)
                finish(e, 7)
                if a is not None:
                    max_q(a, 3)
                if c is not None:
                    did = chain(y_stat, c, Y_STEPS, 0)
                    did(y_bn(c, 3))
                    channel_stats(1, did)
                if a is not None:
                    dve.wait_ge(max_turned, at(a, 2, 2))
                    dve.tensor_copy(qmT[:], small_ps[:, 0:P // 2].bitcast(BF16)).then_inc(q_max, 1)
                if c is not None:
                    dve.wait_ge(y_group, at(c, 1, 1))
                    variance(1, chain(y_stat, c, Y_STEPS, 4))
                    dve.wait_ge(y_stat_act, at(c, 2, 2))
                    scale_shift_y(c)
                if c is not None:
                    for v in range(UNITS):
                        low_part(c, v)
                if p is not None:
                    x_stats(p, True)
                    x_stats(p, False)
                if a is not None:
                    dve.wait_ge(ctx_sum, at(a, UNITS, UNITS))
                    dve.wait_ge(pk_ready, at(a, 1, 1))
                    did = chain(mix_dve, a, 8, 0)
                    did(dve.tensor_tensor(z[:, 0:1], sum_ps[:, P:P + 1], pk_sum[:], ALU.add))
                    did(dve.reciprocal(z[:, 1:2], z[:, 0:1]))
                    did(dve.tensor_scalar(A_sb[:, 0:P], sum_ps[:, 0:P], z[:, 1:2], None, ALU.mult), wait=False)
                    did(dve.tensor_scalar(A_sb[:, P:P + MEM], pk[:], z[:, 1:2], None, ALU.mult), wait=False)
                if p is not None:
                    x_variance(p)
                if a is not None:
                    dve.wait_ge(mix_pe, at(a, 3, 1))
                    did(dve.tensor_copy(AT_sb[:], small_ps[:, 0:P]), wait=False)
                    did(dve.tensor_copy(pkT_sb[0:MEM], small_ps[0:MEM, P:2 * P]), wait=False)
                if p is not None:
                    x_scale(p)
                if a is not None:
                    dve.wait_ge(mix_pe, at(a, 3, 2))
                    did(dve.tensor_tensor(ctxT_sb[:], small_ps[:, 0:P], head_mask[:], ALU.mult), wait=False)
                    dve.wait_ge(den_act, at(a, 2, 2))
                    three_parts(den, R_den, chain(den_dve, a, 4, 0))
                    dve.wait_ge(mix_pe, at(a, 3, 3))
                    did(dve.tensor_copy(MT_sb[:], small_ps[:, 0:P]), wait=False)
                finish(c, 0)
                if a is not None:
                    soften(a, 0)
                    soften(a, 1)
                finish(c, 1)
                if p is not None:
                    norm_guard(p)
                if a is not None:
                    residual(a, 0)
                    residual(a, 1)
                finish(c, 2)
                if a is not None:
                    soften(a, 2)
                    soften(a, 3)
                if p is not None:
                    norm_parts(p)
                if a is not None:
                    residual(a, 2)
                    residual(a, 3)
                finish(c, 3)

            def scale_shift_y(c):
                scale_shift(1, chain(y_stat, c, Y_STEPS, 7))

            x_stats((None, 0), True)
            x_stats((None, 0), False)
            x_variance((None, 0))
            x_scale((None, 0))
            norm_guard((None, 0))
            norm_parts((None, 0))
            over_samples(dve, step)

    return nc


_INS = ['x', 'L0_conv_g', 'L0_conv_w_qkv', 'L0_conv_mem_kv', 'L0_conv_w_out', 'L0_conv_b_out',
        'L1_conv_w3', 'L1_conv_w1', 'L1_conv_b']


def kernel(**inputs):
    import numpy as _np
    import concourse.bacc as _bacc
    from concourse.bass_utils import run_bass_kernel_spmd as _run

    nc = _bacc.Bacc("TRN2", target_bir_lowering=False, num_devices=1)
    arrays, args = {}, []
    for name in _INS:
        a = _np.ascontiguousarray(inputs[name])
        arrays[f"in_{name}"] = a
        args.append(nc.dram_tensor(f"in_{name}", a.shape, mybir.dt.from_np(a.dtype), kind="ExternalInput").ap())
    out = nc.dram_tensor("out", inputs["x"].shape, F32, kind="ExternalOutput").ap()
    build(nc, *args, out)
    r = _run(nc, [arrays], core_ids=[0])
    return r.results[0]["out"]
```

```python
from contextlib import ExitStack

import concourse.bass as bass
from concourse import mybir

ALU = mybir.AluOpType
ACT = mybir.ActivationFunctionType
AX = mybir.AxisListType
F32 = mybir.dt.float32
F16 = mybir.dt.float16
I32 = mybir.dt.int32
BF16 = mybir.dt.bfloat16

P = 128
SIDE = 64
PIX = SIDE * SIDE
BANK = 512
CHUNKS = PIX // BANK
UNIT = 2 * BANK
UNITS = PIX // UNIT
BLOCKS = PIX // P
UB = UNIT // P
RES = 4
HEADS = 4
DH = 32
MEM = 4
PAD = SIDE + 2
ROWS = BANK // SIDE
UROWS = UNIT // SIDE
EARLY = 3
SPLIT = EARLY * ROWS + 2
TAPS = 9
REP_DMAS = RES * 6
GN_EPS = 1e-5
W_SCALE = 64.0
LN_SCALE = 2.0 ** 40
RSQRT_SEED = float(0x5F3759DF)
LN2 = 0.6931471805599453
SMALL_CONSTANTS = 13
POOL_STEPS = 20
BIASES_READY = 5
SETUP_READY = 15
WEIGHT_DMAS = 1 + 4 * RES
COL_DMAS = 2 + 2 * RES
X_STEPS = 17
Y_STEPS = 18


def at(sample, per, n):
    triple, offset = sample
    if triple is None:
        return offset * per + n
    return triple * (3 * per) + (offset * per + n)


def build(nc, x, g, w_qkv, mem_kv, w_out, b_out, w3, w1, b1, out):
    batch = x.shape[0]
    x_dram = x.rearrange("b (i r) h w -> b r i (h w)", r=RES)
    out_dram = out.rearrange("b (i r) h w -> b r i (h w)", r=RES)

    with ExitStack() as ctx:
        ctx.enter_context(nc.allow_low_precision(reason="16-bit types carry shifts of softmaxes and parts of float32 values"))
        ctx.enter_context(nc.allow_non_contiguous_dma(reason="small weights in permuted order"))

        def sb(name, shape, dt=F32):
            return ctx.enter_context(nc.sbuf_tensor(name, shape, dt))

        def sem(name):
            return ctx.enter_context(nc.semaphore(name))

        conv_ps = ctx.enter_context(nc.psum_tensor("conv_ps", [P, 2, BANK], F32))
        sum_ps = ctx.enter_context(nc.psum_tensor("sum_ps", [P, BANK], F32))
        small_ps = ctx.enter_context(nc.psum_tensor("small_ps", [P, BANK], F32))
        pair_ps = [ctx.enter_context(nc.psum_tensor(f"pair{q}_ps", [P, UNIT], F32)) for q in range(2)]

        B = [sb(f"image{q}", [P, PIX]) for q in range(3)]
        U = sb("u", [P, PIX])
        KT = sb("exp_kT", [P, 2, UNIT])
        UH = sb("u_hi", [P, PIX], F16)
        UL = sb("u_lo", [P, PIX], F16)
        SQ = KT
        UT = sb("uT", [P, 2, UB, P + 1])
        EQ = sb("exp_q", [P, PIX])
        YG = EQ
        HI = sb("yg_hi", [P, PAD, PAD], F16)
        LO = sb("yg_lo", [P, PAD, PAD], F16)
        REP = sb("replicas", [P, RES, PAD * PAD], F16)
        LREP = sb("lo_replicas", [P, 2, PAD * PAD], F16)
        bn = sb("bn", [P, CHUNKS, 6])
        y_sums = sb("y_sums", [P, 2, UNITS])
        st = sb("st", [P, 2, 16])
        nrm = sb("nrm", [P, BANK])
        den = nrm
        part = UL[:, 0:BANK].bitcast(BF16)
        R_norm = sb("r_norm", [P, BANK], BF16)
        R_den = UL[:, BANK:2 * BANK].bitcast(BF16)
        km = sb("km", [P, 8])
        kneg_bf = sb("kneg_bf", [P, 2], BF16)
        kneg = sb("kneg", [P, 1])
        krow = sb("krow", [P, 4, P], BF16)
        pk = sb("pk", [P, MEM])
        pk_sum = sb("pk_sum", [P, 1])
        z = sb("z", [P, 2])
        qm = sb("qm", [P, P], BF16)
        qmT = sb("qmT", [P, P], BF16)
        A_sb = sb("a_sb", [P, P + MEM])
        AT_sb = sb("at_sb", [P, P])
        pkT_sb = sb("pkT_sb", [P, P])
        ctxT_sb = sb("ctxT_sb", [P, P])
        MT_sb = sb("mt_sb", [P, P])
        ident = sb("ident", [P, P])
        ident_bf = sb("ident_bf", [P, P], BF16)
        ones_bf = sb("ones_bf", [P, P], BF16)
        same_group = sb("same_group", [P, P])
        head_mask = sb("head_mask", [P, P])
        quad_mask = LREP[:, 0, 0:2 * P].bitcast(F32)
        other_mask = LREP[:, 0, 2 * P:4 * P].bitcast(F32)
        part_grid = LREP[:, 0, 4 * P:6 * P].bitcast(F32).rearrange("p (k t w) -> p k t w", k=4, t=4)
        w_hi = REP[:, 0, 0:TAPS * P].rearrange("p (t o) -> p t o", t=TAPS)
        w_lo = REP[:, 1, 0:TAPS * P].rearrange("p (t o) -> p t o", t=TAPS)
        red_norm = sb("red_norm", [P, 2, 32])
        red_head = sb("red_head", [P, 2, 32])
        spread = sb("spread", [P, CHUNKS, P], BF16)
        minus_max = sb("minus_max", [P, BLOCKS, P], BF16)
        part_mask = sb("part_mask", [P, 4])
        cut = sb("cut", [P, 2])
        mk = sb("mk", [P, MEM])
        mv = sb("mv", [P, MEM])
        mvT = sb("mvT", [P, P])
        wqkvT = sb("wqkvT", [P, 3, P])
        wqk_h = sb("wqk_hi", [P, 2, P], F16)
        wqk_l = sb("wqk_lo", [P, 2, P], F16)
        woT = sb("woT", [P, P])
        gcol = sb("gcol", [P, 1])
        bo = sb("bo", [P, 1])
        b1s = sb("b1s", [P, 1])
        minus_b1 = sb("minus_b1", [P, 1])
        b01 = sb("b01", [P, 1])
        w_rep = sb("w_rep", [P, 2, 3, RES, 32], F16)
        w_lrep = sb("w_lrep", [P, 3, 2, 2, 32], F16)
        w_mid = sb("w_mid", [P, 2, P], F16)
        idle = sb("idle", [P, 10])
        zcol = sb("zcol", [P, 3])

        raw_qkv = EQ[:, 0:3 * P].rearrange("p (t c) -> p t c", t=3)
        raw_out = EQ[:, 3 * P:4 * P]
        raw_b1 = EQ[:, 4 * P:5 * P]
        raw_w1 = EQ[:, 5 * P:6 * P]
        raw_w3 = EQ[:, 6 * P:15 * P]
        perm_qkv = B[2][:, 0:3 * P].rearrange("p (t r i) -> p t r i", t=3, r=RES)
        perm_w3 = B[2][:, 3 * P:12 * P].rearrange("p (t r i) -> p t r i", t=TAPS, r=RES)
        perm_w1 = B[2][:, 12 * P:13 * P].rearrange("p (r i) -> p r i", r=RES)
        tap32 = B[2][:, 13 * P:23 * P].rearrange("p (t c) -> p t c", t=TAPS + 1)

        x_in = [sem(f"x_in{q}") for q in range(3)]
        weights_in = sem("weights_in")
        stored = [sem(f"stored{u}") for u in range(UNITS)]
        rep_in = [sem(f"rep_in{h}") for h in range(2)]
        rep_weights_in = sem("rep_weights_in")
        col_in = sem("col_in")
        const_made = sem("const_made")
        setup_pe = sem("setup_pe")
        setup_dve = sem("setup_dve")
        x_stat = sem("x_stat")
        x_group = sem("x_group")
        y_stat = sem("y_stat")
        y_summed = sem("y_summed")
        y_group = sem("y_group")
        xg_ready = sem("xg_ready")
        sq_ready = sem("sq_ready")
        norm_sum = sem("norm_sum")
        norm_dve = sem("norm_dve")
        norm_act = sem("norm_act")
        inv_bcast = sem("inv_bcast")
        u_ready = sem("u_ready")
        uh_ready = sem("uh_ready")
        ul_ready = sem("ul_ready")
        k_rough = sem("k_rough")
        k_max = sem("k_max")
        q_rough = sem("q_rough")
        q_max = sem("q_max")
        max_turned = sem("max_turned")
        pk_ready = sem("pk_ready")
        kT_done = sem("kT_done")
        uT_done = sem("uT_done")
        kT_exp = sem("kT_exp")
        uT_kept = sem("uT_kept")
        ctx_sum = sem("ctx_sum")
        mix_dve = sem("mix_dve")
        mix_pe = sem("mix_pe")
        q_done = sem("q_done")
        q_exp = sem("q_exp")
        den_sum = sem("den_sum")
        den_act = sem("den_act")
        den_dve = sem("den_dve")
        den_bcast = sem("den_bcast")
        q_soft = sem("q_soft")
        mixed = sem("mixed")
        y_ready = sem("y_ready")
        yg_ready = sem("yg_ready")
        hi_ready = sem("hi_ready")
        lo_ready = sem("lo_ready")
        conv_done = sem("conv_done")
        out_ready = sem("out_ready")

        def px(t, v):
            return t[:, v * UNIT:(v + 1) * UNIT]

        def flat(t):
            return t[:].rearrange("p r c -> p (r c)")

        def inner(t, v):
            return t[:, 1 + v * UROWS:1 + (v + 1) * UROWS, 1:1 + SIDE]

        def rows(ap):
            return ap.rearrange("p (r c) -> p r c", c=SIDE)

        def first(sample):
            return sample[0] is None and sample[1] == 0

        def index(sample):
            triple, offset = sample
            return offset if triple is None else triple * 3 + offset

        def at_load(sample):
            triple, offset = sample
            loads = 16 * RES
            return loads * (offset // 3 + 1) if triple is None else triple * loads + loads * (offset // 3 + 1)

        def buffer_of(sample):
            return sample[1] % 3

        def image(sample):
            return B[buffer_of(sample)]

        def over_samples(eng, step):
            def known(s):
                return (None, s) if 0 <= s < batch else None

            def peeled(s):
                step(known(s), known(s - 1), known(s - 2), known(s + 1))

            for s in range(3):
                peeled(s)
            triples = (batch - 1) // 3
            with eng.Fori(1, triples) as t:
                for k in range(3):
                    step((t, k), (t, k - 1), (t, k - 2), (t, k + 1))
            for s in range(3 * triples, batch + 2):
                peeled(s)

        block = ctx.enter_context(nc.Block())

        @block.sync
        def _(sp):
            def load(s):
                for r in range(RES):
                    sp.dma_start(image(s)[32 * r:32 * r + 32], x_dram[index(s), r]).then_inc(x_in[buffer_of(s)], 16)

            def store(s, v):
                sp.wait_ge(out_ready, at(s, CHUNKS, 2 * v + 2))
                for r in range(RES):
                    sp.dma_start(out_dram[index(s), r][:, v * UNIT:(v + 1) * UNIT],
                                 px(image(s), v)[32 * r:32 * r + 32]).then_inc(stored[v], 16)

            def replicate(s, half, e=None):
                first_col, end_col = (0, SPLIT * PAD - 2) if half == 0 else (SPLIT * PAD, PAD * PAD - 2)
                sp.wait_ge(hi_ready, at(s, UNITS, 2 + 2 * half))
                if e is not None:
                    sp.wait_ge(conv_done, at(e, CHUNKS, CHUNKS))
                elif half == 0:
                    sp.wait_ge(rep_weights_in, 16 * 10 * RES)
                for r in range(RES):
                    for shift in range(3):
                        sp.dma_start(REP[32 * shift:32 * shift + 32, r, first_col:end_col],
                                     flat(HI)[32 * r:32 * r + 32, first_col + shift:end_col + shift]
                                     ).then_inc(rep_in[half], 16)
                sp.wait_ge(lo_ready, at(s, UNITS, 2 + 2 * half))
                for r in range(RES):
                    q = slice(32 * r, 32 * r + 32)
                    sp.dma_start(REP[96:128, r, first_col:end_col],
                                 flat(LO)[q, first_col:end_col]).then_inc(rep_in[half], 16)
                    for shift in (1, 2):
                        start = 64 * (r % 2) + 32 * (shift - 1)
                        sp.dma_start(LREP[start:start + 32, r // 2, first_col:end_col],
                                     flat(LO)[q, first_col + shift:end_col + shift]).then_inc(rep_in[half], 16)

            def replicate_weights():
                sp.wait_ge(setup_dve, SETUP_READY)
                for q in range(4):
                    for r in range(RES):
                        c = slice(32 * r, 32 * r + 32)
                        for part, w in enumerate((w_hi, w_lo)):
                            sp.dma_start(w_rep[32 * q:32 * q + 32, part, :, r, :],
                                          w[c].rearrange("p (dy dx) o -> p dy dx o", dx=3)[:, :, q % 3, c]
                                          ).then_inc(rep_weights_in, 16)
                for r in range(RES):
                    c = slice(32 * r, 32 * r + 32)
                    for shift in (1, 2):
                        start = 64 * (r % 2) + 32 * (shift - 1)
                        sp.dma_start(w_lrep[start:start + 32, :, r // 2, r % 2, :],
                                      w_hi[c].rearrange("p (dy dx) o -> p dy dx o", dx=3)[:, :, shift, c]
                                      ).then_inc(rep_weights_in, 16)

            load((None, 0))
            sp.dma_start(raw_qkv, w_qkv.rearrange("(t o) c -> o t c", t=3)).then_inc(weights_in, 16)
            n = 1
            for r in range(RES):
                q = slice(32 * r, 32 * r + 32)
                sp.dma_start(raw_w3[q], w3.rearrange("(i r) c a b -> r i (c a b)", r=RES)[r]).then_inc(weights_in, 16)
                sp.dma_start(raw_w1[q], w1.rearrange("(i r) c -> r i c", r=RES)[r]).then_inc(weights_in, 16)
                sp.dma_start(raw_b1[q], b1.rearrange("(i r) c -> r i c", r=RES)[r]).then_inc(weights_in, 16)
                sp.dma_start(raw_out[q], w_out.rearrange("(i r) c -> r i c", r=RES)[r]).then_inc(weights_in, 16)
                n += 4
            assert n == WEIGHT_DMAS

            def step(a, c, e, p):
                if e is not None:
                    store(e, 2)
                    store(e, 3)
                if p is not None:
                    if e is not None:
                        for v in range(UNITS):
                            sp.wait_ge(stored[v], at(e, 16 * RES, 16 * RES))
                    elif a[1] == 1:
                        sp.wait_ge(setup_dve, SETUP_READY)
                    load(p)
                if a is not None and c is None:
                    replicate_weights()
                if c is not None:
                    replicate(c, 0, e)
                    replicate(c, 1)
                    store(c, 0)
                    store(c, 1)

            over_samples(sp, step)
            for v in range(UNITS):
                sp.wait_ge(stored[v], 16 * RES * batch)

        @block.gpsimd
        def _(pool):
            made = 0

            def make(ins):
                nonlocal made
                ins.then_inc(const_made, 1)
                made += 1
                pool.wait_ge(const_made, made)

            n = 0
            for r in range(RES):
                q = slice(32 * r, 32 * r + 32)
                pool.dma_start(gcol[q], g.rearrange("(i r one) -> r i one", r=RES, one=1)[r]).then_inc(col_in, 16)
                pool.dma_start(bo[q], b_out.rearrange("(i r one) -> r i one", r=RES, one=1)[r]).then_inc(col_in, 16)
                n += 2
            pool.dma_start(mk[:], mem_kv[0].rearrange("h d j -> (h d) j")).then_inc(col_in, 16)
            pool.dma_start(mv[:], mem_kv[1].rearrange("h d j -> (h d) j")).then_inc(col_in, 16)
            assert n + 2 == COL_DMAS
            make(pool.memset(ident[:], 0.0))
            make(pool.affine_select(out=ident[:], in_=ident[:], compare_op=ALU.not_equal, fill=1.0, base=0,
                                    pattern=[[-1, P]], channel_multiplier=1))
            make(pool.tensor_copy(ident_bf[:], ident[:]))
            make(pool.memset(same_group[:], 0.0))
            for k in range(-(RES - 1), RES):
                make(pool.affine_select(out=same_group[:], in_=same_group[:], compare_op=ALU.not_equal,
                                        fill=1.0 / RES, base=32 * k, pattern=[[-1, P]], channel_multiplier=1))
            make(pool.memset(part_grid[:], 0.0))
            make(pool.affine_select(out=part_grid[:], in_=part_grid[:], compare_op=ALU.not_equal, fill=1.0,
                                    base=0, pattern=[[-8, 4], [-32, 4], [-1, 8]], channel_multiplier=1))
            assert made == SMALL_CONSTANTS
            make(pool.memset(spread[:], 0.0))
            for part_no in range(3):
                make(pool.affine_select(out=spread[:], in_=spread[:], compare_op=ALU.not_equal, fill=1.0,
                                        base=-8 * part_no, pattern=[[-4, 2], [-32, 4], [-1, HEADS], [0, DH]],
                                        channel_multiplier=1))
            make(pool.memset(idle[:, 3:4], 0.0))

            def take_wait(column):
                pool.tensor_tensor(idle[:, column:column + 1], idle[:, 3:4], idle[:, 3:4], ALU.add)

            def group_norm_x(a, p):
                pool.wait_ge(x_stat, at(p, X_STEPS, X_STEPS))
                take_wait(5)
                for v in range(UNITS):
                    if a is not None:
                        pool.wait_ge(uT_done, at(a, UNITS, v + 1))
                        take_wait(6 + v)
                    pool.tensor_scalar(px(U, v), px(image(p), v), st[:, 0, 9:10],
                                       st[:, 0, 10:11], ALU.mult, ALU.add).then_inc(xg_ready, 1)

            def step(a, c, e, p):
                if a is not None:
                    for v in range(UNITS):
                        pool.wait_ge(uh_ready, at(a, UNITS, v + 1))
                        pool.tensor_tensor(px(UL, v), px(U, v), px(UH, v), ALU.subtract).then_inc(ul_ready, 1)
                if c is not None:
                    pool.wait_ge(y_stat, at(c, Y_STEPS, Y_STEPS))
                    take_wait(4)
                    for v in range(UNITS):
                        pool.tensor_scalar(px(YG, v), px(image(c), v), st[:, 1, 9:10], st[:, 1, 11:12],
                                           ALU.mult, ALU.add).then_inc(yg_ready, 1)
                if p is not None:
                    group_norm_x(a, p)

            group_norm_x(None, (None, 0))
            make(pool.memset(minus_max[:], 0.0))
            make(pool.affine_select(out=minus_max[:], in_=minus_max[:], compare_op=ALU.not_equal, fill=-1.0,
                                    base=0, pattern=[[-4, BLOCKS], [-1, HEADS], [0, DH]], channel_multiplier=1))
            assert made == POOL_STEPS
            over_samples(pool, step)

        @block.scalar
        def _(act):
            act.wait_ge(setup_dve, BIASES_READY)

            def square(p, v):
                act.wait_ge(xg_ready, at(p, UNITS, v + 1))
                if v >= 2:
                    act.wait_ge(norm_sum, at(p, UNITS, v - 1))
                act.activation(SQ[:, v % 2], px(U, v), ACT.Square, bias=zcol[:, 0:1]).then_inc(sq_ready, 1)

            def inverse_norm(p):
                act.wait_ge(norm_dve, at(p, 5, 1))
                act.activation(nrm[:], nrm[:], ACT.Ln, scale=LN_SCALE, bias=zcol[:, 0:1]).then_inc(norm_act, 1)
                act.wait_ge(norm_act, at(p, 2, 1))
                act.activation(nrm[:], nrm[:], ACT.Exp, scale=-0.5, bias=zcol[:, 1:2]).then_inc(norm_act, 1)

            def sum_y(s, v):
                act.wait_ge(y_ready, at(s, UNITS, v + 1))
                spare = px(EQ, v).bitcast(BF16)
                act.activation(spare[:, 0:UNIT], px(image(s), v), ACT.Identity, bias=minus_b1[:],
                               accum_out=y_sums[:, 0, v:v + 1]).then_inc(y_summed, 1)
                act.activation(spare[:, UNIT:2 * UNIT], px(image(s), v), ACT.Square, bias=minus_b1[:],
                               accum_out=y_sums[:, 1, v:v + 1]).then_inc(y_summed, 1)

            def high_part(c, e, v):
                if v == 0:
                    act.wait_ge(y_stat, at(c, Y_STEPS, Y_STEPS))
                    if e is not None:
                        act.wait_ge(conv_done, at(e, CHUNKS, CHUNKS))
                act.activation(inner(HI, v), rows(px(image(c), v)), ACT.Identity, scale=st[:, 1, 9:10],
                               bias=st[:, 1, 11:12]).then_inc(hi_ready, 1)

            def step(a, c, e, p):
                if a is not None:
                    for v in range(UNITS):
                        act.wait_ge(u_ready, at(a, UNITS, v + 1))
                        act.activation(px(UH, v), px(U, v), ACT.Copy).then_inc(uh_ready, 1)
                if c is not None:
                    sum_y(c, 2)
                    sum_y(c, 3)
                if a is not None:
                    act.wait_ge(k_max, at(a, 8, 7))
                    act.activation(pk[:], mk[:], ACT.Exp, bias=kneg[:], accum_out=pk_sum[:]).then_inc(pk_ready, 1)
                for v in range(UNITS):
                    if c is not None and v >= 2:
                        high_part(c, e, 2 * v - 4)
                        high_part(c, e, 2 * v - 3)
                    if a is not None:
                        act.wait_ge(kT_done, at(a, UNITS, v + 1))
                        if v >= 2:
                            act.wait_ge(ctx_sum, at(a, UNITS, v - 1))
                        act.activation(KT[:, v % 2], pair_ps[0][:], ACT.Exp, bias=zcol[:, 0:1]).then_inc(kT_exp, 1)
                        act.wait_ge(uT_done, at(a, UNITS, v + 1))
                        act.activation(UT[:, v % 2, :, 0:P], pair_ps[1][:].rearrange("p (b c) -> p b c", c=P),
                                       ACT.Copy).then_inc(uT_kept, 1)
                if a is not None:
                    for v in range(UNITS):
                        act.wait_ge(q_done, at(a, UNITS, v + 1))
                        if c is not None:
                            act.wait_ge(lo_ready, at(c, UNITS, v + 1))
                        act.activation(px(EQ, v), pair_ps[v % 2][:], ACT.Exp, bias=zcol[:, 0:1]).then_inc(q_exp, 1)
                    act.wait_ge(den_sum, at(a, 1, 1))
                    act.activation(den[:], sum_ps[:], ACT.Ln, bias=zcol[:, 0:1]).then_inc(den_act, 1)
                    act.wait_ge(den_act, at(a, 2, 1))
                    act.activation(den[:], den[:], ACT.Exp, scale=-1.0, bias=zcol[:, 0:1]).then_inc(den_act, 1)
                if p is not None:
                    for v in range(UNITS):
                        square(p, v)
                    inverse_norm(p)
                if a is not None:
                    sum_y(a, 0)
                    sum_y(a, 1)

            for v in range(UNITS):
                square((None, 0), v)
            inverse_norm((None, 0))
            over_samples(act, step)

        @block.tensor
        def _(pe):
            pe.wait_ge(const_made, SMALL_CONSTANTS)
            pe.wait_ge(col_in, 16 * COL_DMAS)
            pe.wait_ge(setup_dve, 3)
            def turn(dst, src, m=P):
                return pe.transpose(dst, src, ident[:])
            for t in range(3):
                turn(conv_ps[:, 0, t * P:(t + 1) * P], perm_qkv[:, t].rearrange("p r i -> p (r i)"))
            turn(conv_ps[:, 0, 3 * P:4 * P], raw_out)
            pe.transpose(conv_ps[0:MEM, 1, 0:P], mv[:], ident[:])
            for t in range(TAPS + 1):
                src = perm_w3[:, t] if t < TAPS else perm_w1
                bank = [pair_ps[0][:, 0:BANK], pair_ps[0][:, BANK:UNIT], pair_ps[1][:, 0:BANK]][t // 4]
                last = turn(bank[:, (t % 4) * P:(t % 4 + 1) * P], src.rearrange("p r i -> p (r i)"))
            last.then_inc(setup_pe, 1)

            def norm_sums(p, v):
                pe.wait_ge(sq_ready, at(p, UNITS, v + 1))
                for j in (2 * v, 2 * v + 1):
                    t, s = j % 4, j // 4
                    mm = pe.matmul(sum_ps[32 * t:32 * t + 32, :], red_norm[:, s], SQ[:, v % 2, (j % 2) * BANK:(j % 2 + 1) * BANK],
                                   start=(s == 0), stop=(s == 1))
                mm.then_inc(norm_sum, 1)

            def broadcast(R, v, done):
                for j in (2 * v, 2 * v + 1):
                    mm = pe.matmul(pair_ps[v % 2][:, (j % 2) * BANK:(j % 2 + 1) * BANK], spread[:, j], R[:],
                                   start=True, stop=True)
                mm.then_inc(done, 1)

            def inv_norm(a, c, v):
                if v == 0:
                    pe.wait_ge(norm_dve, at(a, 5, 5))
                if v < 2 and c is not None:
                    pe.wait_ge(y_ready, at(c, UNITS, 3 + v))
                if v >= 2:
                    pe.wait_ge(u_ready, at(a, UNITS, v - 1))
                broadcast(R_norm, v, inv_bcast)

            def rough_k(a, v):
                pe.wait_ge(uh_ready, at(a, UNITS, v + 1))
                if v < 2:
                    pe.wait_ge(u_ready, at(a, UNITS, v + 3))
                else:
                    pe.wait_ge(k_max, at(a, 8, v - 1))
                for j in (2 * v, 2 * v + 1):
                    mm = pe.matmul(pair_ps[v % 2][:, (j % 2) * BANK:(j % 2 + 1) * BANK], wqk_h[:, 1],
                                   UH[:, j * BANK:(j + 1) * BANK], start=True, stop=True)
                mm.then_inc(k_rough, 1)

            def rough_q(a, v):
                if v < 2:
                    pe.wait_ge(k_max, at(a, 8, v + 3))
                else:
                    pe.wait_ge(q_max, at(a, 5, v - 1))
                for b in range(UB):
                    c0 = (v * UB + b) * P
                    mm = pe.matmul(pair_ps[v % 2][:, b * P:(b + 1) * P], UH[:, c0:c0 + P], wqk_h[:, 0],
                                   start=True, stop=True)
                mm.then_inc(q_rough, 1)

            def keys(a, v):
                if v == 0:
                    pe.wait_ge(k_max, at(a, 8, 8))
                    pe.wait_ge(q_max, at(a, 5, 3))
                else:
                    pe.wait_ge(kT_exp, at(a, UNITS, v))
                pe.wait_ge(ul_ready, at(a, UNITS, v + 1))
                for half in range(2):
                    bank = pair_ps[0][:, half * BANK:(half + 1) * BANK]
                    pe.matmul(bank, ones_bf[:], krow[:].rearrange("p a b -> p (a b)"), start=True, stop=False,
                              skip_group_check=True)
                    for b in range(4):
                        c0 = (v * UB + half * 4 + b) * P
                        for n, (u, w) in enumerate(((UH, wqk_h), (UH, wqk_l), (UL, wqk_h))):
                            mm = pe.matmul(bank[:, b * P:(b + 1) * P], u[:, c0:c0 + P], w[:, 1],
                                           start=False, stop=(b == 3 and n == 2), skip_group_check=True)
                mm.then_inc(kT_done, 1)

            def turn_u(a, v):
                if v == 0:
                    pe.wait_ge(q_max, at(a, 5, 4))
                else:
                    pe.wait_ge(uT_kept, at(a, UNITS, v))
                for b in range(UB):
                    c0 = (v * UB + b) * P
                    mm = pe.transpose(pair_ps[1][:, b * P:(b + 1) * P], U[:, c0:c0 + P], ident[:])
                mm.then_inc(uT_done, 1)

            def context(a, v):
                pe.wait_ge(kT_exp, at(a, UNITS, v + 1))
                pe.wait_ge(uT_kept, at(a, UNITS, v + 1))
                for b in range(UB):
                    mm = pe.matmul(sum_ps[:, 0:P + 1], KT[:, v % 2, b * P:(b + 1) * P], UT[:, v % 2, b],
                                   start=(v == 0 and b == 0), stop=(v == UNITS - 1 and b == UB - 1))
                mm.then_inc(ctx_sum, 1)

            def queries(a, v):
                if v == 0:
                    pe.wait_ge(q_max, at(a, 5, 5))
                    pe.wait_ge(kT_exp, at(a, UNITS, UNITS))
                elif v == 1:
                    pe.wait_ge(uT_kept, at(a, UNITS, UNITS))
                else:
                    pe.wait_ge(q_exp, at(a, UNITS, v - 1))
                for j in (2 * v, 2 * v + 1):
                    bank = pair_ps[v % 2][:, (j % 2) * BANK:(j % 2 + 1) * BANK]
                    for n, (w, u) in enumerate(((wqk_h, UH), (wqk_h, UL), (wqk_l, UH))):
                        pe.matmul(bank, w[:, 0], u[:, j * BANK:(j + 1) * BANK], start=(n == 0), stop=False,
                                  skip_group_check=True)
                    for b in range(4):
                        mm = pe.matmul(bank[:, b * P:(b + 1) * P], minus_max[:, 4 * j + b], qmT[:],
                                       start=False, stop=(b == 3), skip_group_check=True)
                mm.then_inc(q_done, 1)

            def denominators(a):
                pe.wait_ge(mix_dve, at(a, 8, 3))
                for j in range(CHUNKS):
                    t, s = j % 4, j // 4
                    if j % 2 == 0:
                        pe.wait_ge(q_exp, at(a, UNITS, j // 2 + 1))
                    mm = pe.matmul(sum_ps[32 * t:32 * t + 32, :], red_head[:, s], EQ[:, j * BANK:(j + 1) * BANK],
                                   start=(s == 0), stop=(s == 1))
                mm.then_inc(den_sum, 1)

            def den_broadcast(a, v):
                if v < 2:
                    if v == 0:
                        pe.wait_ge(den_dve, at(a, 4, 4))
                    pe.wait_ge(q_exp, at(a, UNITS, v + 3))
                else:
                    pe.wait_ge(y_ready, at(a, UNITS, v - 1))
                broadcast(R_den, v, den_bcast)

            def mix(a, v):
                if v == 0:
                    pe.wait_ge(mix_dve, at(a, 8, 8))
                pe.wait_ge(q_soft, at(a, UNITS, v + 1))
                for j in (2 * v, 2 * v + 1):
                    mm = pe.matmul(pair_ps[v % 2][:, (j % 2) * BANK:(j % 2 + 1) * BANK], MT_sb[:],
                                   EQ[:, j * BANK:(j + 1) * BANK], start=True, stop=True)
                mm.then_inc(mixed, 1)

            def conv_dense(s, j):
                if s is None:
                    return
                if j in (0, EARLY):
                    pe.wait_ge(rep_in[j // EARLY], at(s, 16 * REP_DMAS, 16 * REP_DMAS))
                if first(s) and j == 0:
                    pe.wait_ge(rep_weights_in, 16 * 10 * RES)
                if j >= 2 or not first(s):
                    pe.wait_ge(out_ready, at(s, CHUNKS, max(0, j - 1)))
                for n, (w, data) in enumerate(((0, HI), (1, HI), (0, LO))):
                    pe.matmul(conv_ps[:, j % 2], w_mid[:, w], data[:, j * ROWS + 1:(j + 1) * ROWS + 1, 1:1 + SIDE],
                              start=(n == 0), stop=False, skip_group_check=True)
                for dy in range(3):
                    for pair in range(2):
                        rep = LREP[:, pair].rearrange("p (y x) -> p y x", x=PAD)
                        pe.matmul(conv_ps[64 * pair:64 * pair + 64, j % 2],
                                  w_lrep[:, dy, pair].rearrange("p k o -> p (k o)"),
                                  rep[:, j * ROWS + dy:(j + 1) * ROWS + dy, 0:SIDE],
                                  start=False, stop=False, skip_group_check=True)

            def conv_replicas(s, j):
                if s is None:
                    return
                for dy in range(3):
                    for part in range(2):
                        for r in range(RES):
                            rep = REP[:, r].rearrange("p (y x) -> p y x", x=PAD)
                            mm = pe.matmul(conv_ps[32 * r:32 * r + 32, j % 2], w_rep[:, part, dy, r],
                                           rep[:, j * ROWS + dy:(j + 1) * ROWS + dy, 0:SIDE],
                                           start=False, stop=(dy == 2 and part == 1), skip_group_check=True)
                mm.then_inc(conv_done, 1)

            def group_means(src, done):
                pe.matmul(small_ps[:, 0:2], same_group[:], st[:, src, 0:2], start=True, stop=True).then_inc(done, 1)

            def turn_k_max(a, c):
                if c is not None:
                    pe.wait_ge(mix_dve, at(c, 8, 8))
                pe.wait_ge(k_max, at(a, 8, 6))
                pe.transpose(small_ps[0:1, 0:P // 2].bitcast(BF16), kneg_bf[:, 0:1], ident_bf[:]).then_inc(max_turned, 1)

            def turn_q_max(a):
                pe.wait_ge(k_max, at(a, 8, 8))
                pe.wait_ge(q_max, at(a, 5, 4))
                pe.transpose(small_ps[:, 0:P // 2].bitcast(BF16), qm[:], ident_bf[:]).then_inc(max_turned, 1)

            def y_means(a, c):
                if a is not None:
                    pe.wait_ge(q_max, at(a, 5, 5))
                else:
                    pe.wait_ge(mix_dve, at(c, 8, 8))
                pe.wait_ge(y_stat, at(c, Y_STEPS, 2))
                group_means(1, y_group)

            def step(a, c, e, p):
                if a is not None:
                    inv_norm(a, c, 0)
                    inv_norm(a, c, 1)
                conv_dense(e, 4)
                if a is not None:
                    inv_norm(a, c, 2)
                conv_replicas(e, 4)
                if a is not None:
                    inv_norm(a, c, 3)
                conv_dense(e, 5)
                if a is not None:
                    rough_k(a, 0)
                    rough_k(a, 1)
                conv_replicas(e, 5)
                if a is not None:
                    rough_k(a, 2)
                conv_dense(e, 6)
                if a is not None:
                    rough_k(a, 3)
                conv_replicas(e, 6)
                if a is not None:
                    rough_q(a, 0)
                conv_dense(e, 7)
                if a is not None:
                    rough_q(a, 1)
                    turn_k_max(a, c)
                    rough_q(a, 2)
                conv_replicas(e, 7)
                if a is not None:
                    rough_q(a, 3)
                    for v in range(UNITS):
                        keys(a, v)
                        if v == 0:
                            turn_q_max(a)
                        if v == 1 and c is not None:
                            y_means(a, c)
                        turn_u(a, v)
                        if v > 0:
                            context(a, v - 1)
                    queries(a, 0)
                    context(a, 3)
                    queries(a, 1)
                if p is not None:
                    pe.wait_ge(x_stat, at(p, X_STEPS, 3))
                    if c is not None:
                        pe.wait_ge(y_stat, at(c, Y_STEPS, 3))
                    else:
                        pe.wait_ge(q_max, at(a, 5, 5))
                    group_means(0, x_group)
                if a is not None:
                    queries(a, 2)
                    pe.wait_ge(mix_dve, at(a, 8, 4))
                    if p is not None:
                        pe.wait_ge(x_stat, at(p, X_STEPS, 4))
                    elif c is not None:
                        pe.wait_ge(y_stat, at(c, Y_STEPS, 3))
                    pe.transpose(small_ps[:, 0:P], A_sb[:, 0:P], ident[:])
                    pe.transpose(small_ps[0:MEM, P:2 * P], A_sb[:, P:P + MEM], ident[:]).then_inc(mix_pe, 1)
                    queries(a, 3)
                    pe.wait_ge(mix_dve, at(a, 8, 6))
                    pe.matmul(small_ps[:, 0:P], wqkvT[:, 2], AT_sb[:], start=True, stop=False)
                    pe.matmul(small_ps[:, 0:P], mvT[0:MEM], pkT_sb[0:MEM], start=False, stop=True).then_inc(mix_pe, 1)
                    denominators(a)
                if a is None and c is not None:
                    y_means(a, c)
                conv_dense(c, 0)
                conv_replicas(c, 0)
                if a is not None:
                    pe.wait_ge(mix_dve, at(a, 8, 7))
                    pe.matmul(small_ps[:, 0:P], ctxT_sb[:], woT[:], start=True, stop=True).then_inc(mix_pe, 1)
                conv_dense(c, 1)
                if p is not None:
                    pe.wait_ge(den_act, at(a, 2, 1))
                    norm_sums(p, 0)
                    norm_sums(p, 1)
                conv_replicas(c, 1)
                if a is not None:
                    den_broadcast(a, 0)
                    den_broadcast(a, 1)
                conv_dense(c, 2)
                if p is not None:
                    norm_sums(p, 2)
                    norm_sums(p, 3)
                if a is not None:
                    mix(a, 0)
                    mix(a, 1)
                conv_replicas(c, 2)
                if a is not None:
                    den_broadcast(a, 2)
                    den_broadcast(a, 3)
                conv_dense(c, 3)
                if a is not None:
                    mix(a, 2)
                    mix(a, 3)
                conv_replicas(c, 3)

            pe.wait_ge(x_stat, 3)
            group_means(0, x_group)
            pe.wait_ge(setup_dve, SETUP_READY)
            pe.wait_ge(const_made, POOL_STEPS)
            for v in range(UNITS):
                norm_sums((None, 0), v)
            over_samples(pe, step)

        @block.vector
        def _(dve):
            made = 0

            def make(ins, wait=False):
                nonlocal made
                ins.then_inc(setup_dve, 1)
                made += 1
                if wait:
                    dve.wait_ge(setup_dve, made)

            def chain(sem_, sample, per, n):
                def did(ins, wait=True):
                    nonlocal n
                    ins.then_inc(sem_, 1)
                    n += 1
                    if wait:
                        dve.wait_ge(sem_, at(sample, per, n))
                return did

            def channel_stats(did):
                dve.memset(idle[:, 2:3], 0.0)
                did(dve.bn_aggr(st[:, 0, 0:2], bn[:].rearrange("p c s -> p (c s)")))
                did(dve.scalar_tensor_tensor(out=st[:, 0, 1:2], in0=st[:, 0, 0:1], scalar=st[:, 0, 0:1],
                                             in1=st[:, 0, 1:2], op0=ALU.mult, op1=ALU.add), wait=False)

            def variance(slot, did):
                did(dve.tensor_copy(st[:, slot, 2:4], small_ps[:, 0:2]))
                did(dve.scalar_tensor_tensor(out=st[:, slot, 4:5], in0=st[:, slot, 2:3], scalar=st[:, slot, 2:3],
                                             in1=st[:, slot, 3:4], op0=ALU.mult, op1=ALU.subtract))
                did(dve.tensor_scalar(st[:, slot, 5:6], st[:, slot, 4:5], -1.0, GN_EPS, ALU.mult, ALU.add))

            def scale_shift(slot, did):
                did(dve.tensor_scalar(st[:, slot, 6:7].bitcast(I32), st[:, slot, 5:6].bitcast(I32), -0.5, RSQRT_SEED,
                                      ALU.mult, ALU.add))
                old = 6
                for new in (7, 6, 9):
                    did(dve.scalar_tensor_tensor(out=st[:, slot, 8:9], in0=st[:, slot, old:old + 1],
                                                 scalar=st[:, slot, old:old + 1], in1=st[:, slot, 5:6],
                                                 op0=ALU.mult, op1=ALU.mult))
                    did(dve.tensor_scalar(st[:, slot, 8:9], st[:, slot, 8:9], -0.5, 1.5, ALU.mult, ALU.add))
                    did(dve.tensor_tensor(st[:, slot, new:new + 1], st[:, slot, 8:9], st[:, slot, old:old + 1], ALU.mult))
                    old = new
                did(dve.tensor_scalar(st[:, slot, 10:11], st[:, slot, 2:3], st[:, slot, 9:10], -1.0,
                                      ALU.mult, ALU.mult), wait=(slot == 1))
                if slot == 1:
                    did(dve.tensor_scalar(st[:, slot, 12:13], b1s[:], st[:, slot, 9:10], -1.0, ALU.mult, ALU.mult))
                    did(dve.tensor_tensor(st[:, slot, 11:12], st[:, slot, 12:13], st[:, slot, 10:11], ALU.add), wait=False)

            def x_stats(p, first):
                if first:
                    dve.wait_ge(x_in[buffer_of(p)], at_load(p))
                for j in range(0 if first else 4, 4 if first else CHUNKS):
                    last = dve.bn_stats(bn[:, j], image(p)[:, j * BANK:(j + 1) * BANK])
                if not first:
                    did = chain(x_stat, p, X_STEPS, 0)
                    did(last)
                    channel_stats(did)

            def x_variance(p):
                dve.wait_ge(x_group, at(p, 1, 1))
                variance(0, chain(x_stat, p, X_STEPS, 3))

            def x_scale(p):
                scale_shift(0, chain(x_stat, p, X_STEPS, 6))

            def three_parts(src, R, did):
                did(dve.tensor_copy(part[:], src[:]))
                did(dve.scalar_tensor_tensor(out=src[:], in0=part[:], scalar=cut[:, 0:1], in1=src[:],
                                             op0=ALU.mult, op1=ALU.add))
                did(dve.tensor_copy(part[:], src[:]))
                did(dve.scalar_tensor_tensor(out=R[:], in0=part[:], scalar=cut[:, 1:2], in1=src[:],
                                             op0=ALU.mult, op1=ALU.add), wait=False)

            def norm_guard(p):
                dve.wait_ge(norm_sum, at(p, UNITS, UNITS))
                dve.tensor_scalar(nrm[:], sum_ps[:], 1e-24, None, ALU.max).then_inc(norm_dve, 1)

            def norm_parts(p):
                dve.wait_ge(norm_act, at(p, 2, 2))
                three_parts(nrm, R_norm, chain(norm_dve, p, 5, 1))

            def normalise(a, v):
                dve.wait_ge(inv_bcast, at(a, UNITS, v + 1))
                dve.tensor_tensor(px(U, v), px(U, v), pair_ps[v % 2][:], ALU.mult).then_inc(u_ready, 1)

            def low_part(c, v):
                dve.wait_ge(yg_ready, at(c, UNITS, v + 1))
                dve.wait_ge(hi_ready, at(c, UNITS, v + 1))
                dve.tensor_tensor(inner(LO, v), rows(px(YG, v)), inner(HI, v), ALU.subtract).then_inc(lo_ready, 1)

            def max_k(a, v):
                dve.wait_ge(k_rough, at(a, UNITS, v + 1))
                dve.tensor_reduce(km[:, v:v + 1], pair_ps[v % 2][:], AX.X, ALU.max).then_inc(k_max, 1)

            def max_q(a, v):
                dve.wait_ge(q_rough, at(a, UNITS, v + 1))
                dve.tensor_reduce(qm[:, v * 32:(v + 1) * 32], pair_ps[v % 2][:].rearrange("p (b d) -> p b d", d=DH),
                                  AX.X, ALU.max).then_inc(q_max, 1)

            def finish(s, j):
                if s is None:
                    return
                chunk = image(s)[:, j * BANK:(j + 1) * BANK]
                dve.wait_ge(conv_done, at(s, CHUNKS, j + 1))
                dve.scalar_tensor_tensor(out=chunk, in0=conv_ps[:, j % 2], scalar=1.0 / W_SCALE, in1=chunk,
                                         op0=ALU.mult, op1=ALU.add).then_inc(out_ready, 1)

            def soften(a, v):
                dve.wait_ge(den_bcast, at(a, UNITS, v + 1))
                dve.tensor_tensor(px(EQ, v), px(EQ, v), pair_ps[v % 2][:], ALU.mult).then_inc(q_soft, 1)

            def residual(a, v):
                dve.wait_ge(mixed, at(a, UNITS, v + 1))
                unit = px(image(a), v)
                dve.scalar_tensor_tensor(out=unit, in0=pair_ps[v % 2][:], scalar=b01[:], in1=unit,
                                         op0=ALU.add, op1=ALU.add).then_inc(y_ready, 1)

            def step(a, c, e, p):
                if a is not None:
                    normalise(a, 0)
                    normalise(a, 1)
                    normalise(a, 2)
                finish(e, 4)
                if a is not None:
                    normalise(a, 3)
                if a is not None:
                    max_k(a, 0)
                    max_k(a, 1)
                finish(e, 5)
                if a is not None:
                    max_k(a, 2)
                    max_k(a, 3)
                    did = chain(k_max, a, 8, 4)
                    dve.wait_ge(k_max, at(a, 8, 4))
                    did(dve.tensor_reduce(km[:, 5:6], km[:, 0:5], AX.X, ALU.max))
                    did(dve.tensor_scalar(kneg_bf[:, 0:1], km[:, 5:6], -1.0, None, ALU.mult))
                    did(dve.tensor_copy(kneg[:], kneg_bf[:, 0:1]), wait=False)
                finish(e, 6)
                if a is not None:
                    max_q(a, 0)
                    max_q(a, 1)
                    dve.wait_ge(max_turned, at(a, 2, 1))
                    dve.tensor_copy(krow[0:1], small_ps[0:1, 0:P // 2].bitcast(BF16).unsqueeze(1).to_broadcast([1, 4, P])
                                    ).then_inc(k_max, 1)
                    max_q(a, 2)
                finish(e, 7)
                if a is not None:
                    max_q(a, 3)
                if c is not None:
                    did = chain(y_stat, c, Y_STEPS, 0)
                    dve.wait_ge(y_summed, at(c, 2 * UNITS, 2 * UNITS))
                    did(dve.tensor_reduce(st[:, 1, 0:2], y_sums[:], AX.X, ALU.add))
                    did(dve.tensor_scalar(st[:, 1, 0:2], st[:, 1, 0:2], 1.0 / PIX, None, ALU.mult), wait=False)
                if a is not None:
                    dve.wait_ge(max_turned, at(a, 2, 2))
                    dve.tensor_copy(qmT[:], small_ps[:, 0:P // 2].bitcast(BF16)).then_inc(q_max, 1)
                if c is not None:
                    dve.wait_ge(y_group, at(c, 1, 1))
                    variance(1, chain(y_stat, c, Y_STEPS, 2))
                    scale_shift_y(c)
                if c is not None:
                    for v in range(UNITS):
                        low_part(c, v)
                if p is not None:
                    x_stats(p, True)
                    x_stats(p, False)
                if a is not None:
                    dve.wait_ge(ctx_sum, at(a, UNITS, UNITS))
                    dve.wait_ge(pk_ready, at(a, 1, 1))
                    did = chain(mix_dve, a, 8, 0)
                    did(dve.tensor_tensor(z[:, 0:1], sum_ps[:, P:P + 1], pk_sum[:], ALU.add))
                    did(dve.reciprocal(z[:, 1:2], z[:, 0:1]))
                    did(dve.tensor_scalar(A_sb[:, 0:P], sum_ps[:, 0:P], z[:, 1:2], None, ALU.mult), wait=False)
                    did(dve.tensor_scalar(A_sb[:, P:P + MEM], pk[:], z[:, 1:2], None, ALU.mult), wait=False)
                if p is not None:
                    x_variance(p)
                if a is not None:
                    dve.wait_ge(mix_pe, at(a, 3, 1))
                    did(dve.tensor_copy(AT_sb[:], small_ps[:, 0:P]), wait=False)
                    did(dve.tensor_copy(pkT_sb[0:MEM], small_ps[0:MEM, P:2 * P]), wait=False)
                if p is not None:
                    x_scale(p)
                if a is not None:
                    dve.wait_ge(mix_pe, at(a, 3, 2))
                    did(dve.tensor_tensor(ctxT_sb[:], small_ps[:, 0:P], head_mask[:], ALU.mult), wait=False)
                    dve.wait_ge(den_act, at(a, 2, 2))
                    three_parts(den, R_den, chain(den_dve, a, 4, 0))
                    dve.wait_ge(mix_pe, at(a, 3, 3))
                    did(dve.tensor_copy(MT_sb[:], small_ps[:, 0:P]), wait=False)
                finish(c, 0)
                if a is not None:
                    soften(a, 0)
                    soften(a, 1)
                finish(c, 1)
                if p is not None:
                    norm_guard(p)
                if a is not None:
                    residual(a, 0)
                    residual(a, 1)
                finish(c, 2)
                if a is not None:
                    soften(a, 2)
                    soften(a, 3)
                if p is not None:
                    norm_parts(p)
                if a is not None:
                    residual(a, 2)
                    residual(a, 3)
                finish(c, 3)

            def scale_shift_y(c):
                scale_shift(1, chain(y_stat, c, Y_STEPS, 5))

            dve.wait_ge(weights_in, 16 * WEIGHT_DMAS)
            make(dve.tensor_copy(perm_qkv, raw_qkv.rearrange("p t (i r) -> p t r i", r=RES)))
            make(dve.tensor_copy(perm_w1, raw_w1.rearrange("p (i r) -> p r i", r=RES)))
            for t in range(TAPS):
                last = dve.tensor_copy(perm_w3[:, t], raw_w3.rearrange("p (i r t) -> p t r i", r=RES, t=TAPS)[:, t])
            make(last)
            for t in (ones_bf, UT):
                dve.memset(t[:], 1.0)
            for t in (w_lrep, HI, LO, krow, head_mask, quad_mask, red_norm, red_head):
                last = dve.memset(t[:], 0.0)
            make(last, wait=True)
            dve.memset(other_mask[:], 1.0)
            for h in range(HEADS):
                q = slice(DH * h, DH * h + DH)
                dve.memset(head_mask[q, q], DH ** -0.5)
                dve.memset(quad_mask[q, q], 1.0)
            for s in range(2):
                dve.memset(red_norm[:, s].rearrange("p (part s h) -> p part s h", s=2, h=4)[:, :, s, :], 1.0)
                for h in range(HEADS):
                    q = slice(DH * h, DH * h + DH)
                    dve.memset(red_head[q, s].rearrange("p (part s h) -> p part s h", s=2, h=4)[:, :, s, h:h + 1], 1.0)
            dve.memset(zcol[:, 0:1], 0.0)
            dve.memset(zcol[:, 1:2], 0.5 * (7 + 40) * LN2)
            last = dve.tensor_reduce(b1s[:], raw_b1, AX.X, ALU.add)
            make(last, wait=True)
            for h in range(HEADS):
                q = slice(DH * h, DH * h + DH)
                last = dve.memset(other_mask[q, q], 0.0)
            make(last, wait=True)
            x_stats((None, 0), True)
            x_stats((None, 0), False)
            dve.wait_ge(const_made, SMALL_CONSTANTS)
            make(dve.tensor_reduce(part_mask[:], part_grid[:].rearrange("p k t w -> p k (t w)"), AX.X, ALU.add), wait=True)
            dve.tensor_scalar(cut[:, 0:1], part_mask[:, 0:1], -1.0, None, ALU.add)
            dve.tensor_scalar(cut[:, 1:2], part_mask[:, 2:3], -1.0, None, ALU.mult)
            x_variance((None, 0))
            x_scale((None, 0))
            dve.wait_ge(col_in, 16 * COL_DMAS)
            dve.tensor_tensor(b01[:], bo[:], b1s[:], ALU.add)
            dve.tensor_scalar(minus_b1[:], b1s[:], -1.0, None, ALU.mult)
            make(dve.tensor_reduce(km[:, 4:5], mk[:], AX.X, ALU.max))
            dve.wait_ge(setup_pe, 1)
            make(dve.tensor_scalar(wqkvT[:].rearrange("p t c -> p (t c)"), conv_ps[:, 0, 0:3 * P], gcol[:], None,
                                   ALU.mult), wait=True)
            make(dve.tensor_copy(wqk_h[:], wqkvT[:, 0:2]), wait=True)
            dve.tensor_tensor(wqk_l[:], wqkvT[:, 0:2], wqk_h[:], ALU.subtract)
            dve.tensor_copy(woT[:], conv_ps[:, 0, 3 * P:4 * P])
            dve.tensor_copy(mvT[0:MEM], conv_ps[0:MEM, 1, 0:P])
            for t in range(TAPS + 1):
                bank = [pair_ps[0][:, 0:BANK], pair_ps[0][:, BANK:UNIT], pair_ps[1][:, 0:BANK]][t // 4]
                last = dve.scalar_tensor_tensor(out=tap32[:, t], in0=bank[:, (t % 4) * P:(t % 4 + 1) * P], scalar=W_SCALE,
                                                in1=quad_mask[:] if t < TAPS else other_mask[:],
                                                op0=ALU.mult, op1=ALU.mult)
            make(last, wait=True)
            make(dve.tensor_copy(w_hi[:], tap32[:, 0:TAPS]), wait=True)
            make(dve.tensor_tensor(w_lo[:], tap32[:, 0:TAPS], w_hi[:], ALU.subtract), wait=True)
            make(dve.tensor_copy(w_mid[:, 0], tap32[:, TAPS]), wait=True)
            make(dve.tensor_tensor(w_mid[:, 1], tap32[:, TAPS], w_mid[:, 0], ALU.subtract), wait=True)
            assert made == SETUP_READY, made

            norm_guard((None, 0))
            norm_parts((None, 0))
            over_samples(dve, step)

    return nc


_INS = ['x', 'L0_conv_g', 'L0_conv_w_qkv', 'L0_conv_mem_kv', 'L0_conv_w_out', 'L0_conv_b_out',
        'L1_conv_w3', 'L1_conv_w1', 'L1_conv_b']


def kernel(**inputs):
    import numpy as _np
    import concourse.bacc as _bacc
    from concourse.bass_utils import run_bass_kernel_spmd as _run

    nc = _bacc.Bacc("TRN2", target_bir_lowering=False, num_devices=1)
    arrays, args = {}, []
    for name in _INS:
        a = _np.ascontiguousarray(inputs[name])
        arrays[f"in_{name}"] = a
        args.append(nc.dram_tensor(f"in_{name}", a.shape, mybir.dt.from_np(a.dtype), kind="ExternalInput").ap())
    out = nc.dram_tensor("out", inputs["x"].shape, F32, kind="ExternalOutput").ap()
    build(nc, *args, out)
    r = _run(nc, [arrays], core_ids=[0])
    return r.results[0]["out"]
```
